# Optimizing a Trainium2 kernel written in Bass

```python
import numpy as np
import jax
import jax.numpy as jnp

def _softmax(x, axis=-1):
    return jax.nn.softmax(x, axis=axis)

def _gelu(x):
    return jax.nn.gelu(x, approximate=True)

def _silu(x):
    return jax.nn.silu(x)

def _sigmoid(x):
    return jax.nn.sigmoid(x)

def _layernorm(x, axis=-1, eps=1e-05):
    m = jnp.mean(x, axis=axis, keepdims=True)
    v = jnp.var(x, axis=axis, keepdims=True)
    return (x - m) / jnp.sqrt(v + eps)

def _scatter_add(tgt, idx, src, axis=0):
    return tgt.at[idx].add(src)

def _segment_sum(src, seg, n):
    return jax.ops.segment_sum(src, seg, n)
kernel_name = 'mk_xattn_seq_d1_seqx_r8_237627'

def setup_inputs(seed: int=0):
    np.random.seed(seed)
    _w = jnp.asarray

    def _rec_inputs():
        import jax
        import jax.numpy as jnp
        _rk = jax.random.key(seed)
        x = -0.0002928 + 1 * jax.random.normal(jax.random.fold_in(_rk, 1), (64, 64, 256), jnp.float32)
        _lenS = 64 - jax.random.randint(jax.random.fold_in(_rk, 7), (64,), 0, max(1, 64 // 4) + 1, jnp.int32)
        _lenS2 = 64 - jax.random.randint(jax.random.fold_in(_rk, 8), (64,), 0, max(1, 64 // 4) + 1, jnp.int32)
        _ctx_2048P = jax.random.normal(jax.random.fold_in(_rk, 11), (64, 16, 256), jnp.float32)
        _ctx_2048c = jax.random.dirichlet(jax.random.fold_in(_rk, 511), 0.3 * jnp.ones((16,), jnp.float32), (64, 64))
        _ctx_2048t = jnp.einsum('bsk,bkd->bsd', _ctx_2048c, _ctx_2048P)
        _ctx_2048t = _ctx_2048t * jax.lax.rsqrt(jnp.mean(jnp.square(_ctx_2048t)) + 1e-12) * 0.953939
        ctx_2048 = -1.39393e-06 + 0.999914 * (_ctx_2048t + 0.3 * jax.random.normal(jax.random.fold_in(_rk, 611), (64, 64, 256), jnp.float32))
        return (x, ctx_2048)
    x, ctx_2048 = _rec_inputs()

    def _L0_xattn_setup():
        import jax, jax.numpy as jnp
        import numpy as np
        N, C, S, S2, H, CTX = (4, 64, 256, 256, 8, 64)
        EPS = 1e-05
        key = jax.random.key(seed)
        ks = jax.random.split(key, 6)
        sd = lambda fan: 1.0 / np.sqrt(fan)
        return {'input': jax.random.normal(ks[0], (N, C, S), jnp.float32), 'context': jax.random.normal(ks[1], (N, CTX, S2), jnp.float32), 'gamma': jnp.ones((C,), jnp.float32), 'beta': jnp.zeros((C,), jnp.float32), 'Wq': jax.random.normal(ks[2], (C * H, C), jnp.float32) * sd(C), 'bq': jnp.zeros((C * H,), jnp.float32), 'Wkv': jax.random.normal(ks[3], (C * H * 2, CTX), jnp.float32) * sd(CTX), 'bkv': jnp.zeros((C * H * 2,), jnp.float32), 'Wo': jax.random.normal(ks[4], (C, C * H), jnp.float32) * sd(C * H), 'bo': jnp.zeros((C,), jnp.float32)}
    _L0_xattn_all = _L0_xattn_setup()
    _L0_xattn_in = {k: v for k, v in _L0_xattn_all.items() if k in ('gamma', 'beta', 'Wq', 'bq', 'Wkv', 'bkv', 'Wo', 'bo')}
    del _L0_xattn_all
    return {'x': x, 'ctx_2048': ctx_2048, 'L0_xattn_gamma': _L0_xattn_in['gamma'], 'L0_xattn_beta': _L0_xattn_in['beta'], 'L0_xattn_Wq': _L0_xattn_in['Wq'], 'L0_xattn_bq': _L0_xattn_in['bq'], 'L0_xattn_Wkv': _L0_xattn_in['Wkv'], 'L0_xattn_bkv': _L0_xattn_in['bkv'], 'L0_xattn_Wo': _L0_xattn_in['Wo'], 'L0_xattn_bo': _L0_xattn_in['bo']}

def reference(x, ctx_2048, L0_xattn_gamma, L0_xattn_beta, L0_xattn_Wq, L0_xattn_bq, L0_xattn_Wkv, L0_xattn_bkv, L0_xattn_Wo, L0_xattn_bo):
    import jax
    import jax.numpy as jnp

    def _L0_xattn_ref(input, context, gamma, beta, Wq, bq, Wkv, bkv, Wo, bo):
        import jax, jax.numpy as jnp
        import numpy as np
        N, C, S, S2, H, CTX = (4, 64, 256, 256, 8, 64)
        EPS = 1e-05
        n, c, s = input.shape
        h = H
        mu = jnp.mean(input, axis=(1, 2), keepdims=True)
        var = jnp.var(input, axis=(1, 2), keepdims=True)
        xn = (input - mu) * jax.lax.rsqrt(var + EPS)
        xn = xn * gamma[None, :, None] + beta[None, :, None]
        q = jnp.einsum('oc,ncs->nos', Wq, xn) + bq[None, :, None]
        kv = jnp.einsum('od,nds->nos', Wkv, context) + bkv[None, :, None]
        q = q.reshape(n, h, c, s).transpose(0, 1, 3, 2)
        kv = kv.reshape(n, 2 * h, c, -1).transpose(0, 1, 3, 2)
        k, v = (kv[:, :h], kv[:, h:])
        scale = c ** (-0.25)
        att = jax.nn.softmax(jnp.einsum('nhqc,nhkc->nhqk', q * scale, k * scale), axis=-1)
        y = jnp.einsum('nhqk,nhkc->nhqc', att, v)
        y = y.transpose(0, 1, 3, 2).reshape(n, h * c, s)
        out = jnp.einsum('co,nos->ncs', Wo, y) + bo[None, :, None]
        return input + out
    x = _L0_xattn_ref(x, ctx_2048, L0_xattn_gamma, L0_xattn_beta, L0_xattn_Wq, L0_xattn_bq, L0_xattn_Wkv, L0_xattn_bkv, L0_xattn_Wo, L0_xattn_bo)
    return x

_drawn_inputs = setup_inputs


def setup_inputs(seed=0):
    import zlib

    import numpy as np

    out = dict(_drawn_inputs(seed))
    spreads = {'L0_xattn_gamma': (1.0, 0.2),
     'L0_xattn_beta': (0.0, 0.1),
     'L0_xattn_bq': (0.0, 0.1),
     'L0_xattn_bkv': (0.0, 0.1),
     'L0_xattn_bo': (0.0, 0.1)}
    factors = {}
    for name, (base, spread) in spreads.items():
        noise = np.random.default_rng([zlib.crc32(name.encode()), seed]).standard_normal(out[name].shape)
        drawn = base * np.exp(spread * noise) if base else spread * noise
        out[name] = jnp.asarray(drawn.astype(out[name].dtype))
    for name, factor in factors.items():
        out[name] = (out[name] * factor).astype(out[name].dtype)
    return out
```

```python
from contextlib import ExitStack

import concourse.bass as bass
from concourse import mybir

F32 = mybir.dt.float32
F32R = mybir.dt.float32r
ALU = mybir.AluOpType
ACT = mybir.ActivationFunctionType
AX = mybir.AxisListType

B, C, S = 64, 64, 256
K, CK = 256, 64
H = 8
EPS = 1e-5
SCALE = float(C) ** -0.5

PS = 2
NPAIR = B // PS
UNITS = PS * H
QT = S // 128
KT = K // 128
HP = H // 2

LEAD = 3
FILL_BANKS = 4
PT_BANKS = 2
PROBS = 8
PROBS_T = 8

PROJ_STEP = [6, 7, 8, 10, 11, 12, 14, 15]
MEAN_STEP, VAR_STEP = 2, 3
OUT_STEP = UNITS + 4
CTX_T_STEP = 9
DVE_EVACS = frozenset([1, 5, 9, 13])

FILLS = []
for _u in range(UNITS):
    FILLS.append(("scores", _u + LEAD))
    FILLS += [("proj", _h) for _h in range(H) if PROJ_STEP[_h] == _u]
NFILL = len(FILLS)
assert NFILL % FILL_BANKS == 0


def bank_of(kind, item):
    return FILLS.index((kind, item)) % FILL_BANKS


class Pair:

    def __init__(self, j, c):
        self.j, self.c = j, c

    def shift(self, n):
        return Pair(self.j, self.c + n)

    def exists(self):
        return not isinstance(self.j, int) or 0 <= self.c < NPAIR

    def parity(self):
        return self.c % 2

    def count(self, per_pair, k):
        return self.j * (2 * per_pair) + (per_pair * self.c + k)

    def dma_count(self, k):
        return self.j * 16 + 16 * (self.c // 2 + k)

    def rows(self):
        return self.j * (2 * PS) + PS * self.c


def of_step(pair, item):
    return (pair.shift(item // UNITS), item % UNITS)


def wait(eng, sem, value):
    if not isinstance(value, int) or value > 0:
        eng.wait_ge(sem, value)


def walk(eng, steps):
    steps(Pair(0, -1))
    steps(Pair(0, 0))
    with eng.Fori(0, (NPAIR - 2) // 2) as j:
        steps(Pair(j, 1))
        steps(Pair(j, 2))
    steps(Pair(0, NPAIR - 1))
    steps(Pair(0, NPAIR))


def build(nc, x, ctx, gamma, beta, Wq, bq, Wkv, bkv, Wo, bo, out):
    stack = ExitStack()
    with stack:
        def sb(name, shape, dt=F32):
            return stack.enter_context(nc.sbuf_tensor(name, shape, dt))

        def pb(name, shape):
            return stack.enter_context(nc.psum_tensor(name, shape, F32))

        def sem(name):
            return stack.enter_context(nc.semaphore(name))

        wq2 = sb("wq2", [128, HP, 2, C])
        wk2 = sb("wk2", [128, HP, 2, CK])
        wv = sb("wv", [128, HP, CK])
        wo = sb("wo", [C, H * C])
        bq_cols = sb("bq_cols", [128, HP, 2])
        bv_col = sb("bv_col", [128, HP])
        bo2 = sb("bo2", [128, 1])
        gamma2 = sb("gamma2", [128, 1])
        beta_col = sb("beta_col", [C, 1])
        gamma_scaled = sb("gamma_scaled", [128, 1])
        qk = sb("qk", [C, H, 2 * CK])
        qk_gamma = sb("qk_gamma", [128, H, 2 * CK])
        w_straight = sb("w_straight", [128, H, 2 * CK], F32R)
        w_crossed = sb("w_crossed", [128, H, 2 * CK], F32R)
        d_part = sb("d_part", [128, H])
        d_col = sb("d_col", [128, H])
        wo_t2 = sb("wo_t2", [128, HP, 2, C])
        u_t = sb("u_t", [128, HP, C])
        out_bias = sb("out_bias", [128, 1])
        ident = sb("ident", [128, 128])
        ones = sb("ones", [128, 128])
        minus_half = sb("minus_half", [128, PS])
        x2 = [sb(f"x2_{i}", [128, PS, S]) for i in range(2)]
        c2 = [sb(f"c2_{i}", [128, PS, K]) for i in range(2)]
        x_res = [sb(f"x_res_{i}", [128, S]) for i in range(2)]
        moments = sb("moments", [128, PS, 6])
        mean_var = sb("mean_var", [128, PS, 2])
        mean = sb("mean", [128, PS])
        centred = sb("centred", [128, PS])
        squared = sb("squared", [128, PS])
        spread = sb("spread", [128, PS])
        variance = sb("variance", [128, PS])
        rstd = sb("rstd", [128, PS])
        xhat = sb("xhat", [128, PS, S])
        x_stack = sb("x_stack", [128, PS, S], F32R)
        c_straight = [sb(f"c_straight_{i}", [128, PS, K], F32R) for i in range(2)]
        c_crossed = [sb(f"c_crossed_{i}", [128, PS, K], F32R) for i in range(2)]
        ctx_t = [sb(f"ctx_t_{i}", [128, PS, KT, CK]) for i in range(2)]
        t_stack = sb("t_stack", [128, H, PS, S], F32R)
        neg_max = sb("neg_max", [128, UNITS, QT])
        denom = sb("denom", [128, UNITS, QT])
        recip = sb("recip", [128, UNITS, QT])
        probs = sb("probs", [128, PROBS, QT, K])
        probs_t = sb("probs_t", [128, PROBS_T, KT, S])
        z = sb("z", [128, HP, PS, S])
        y = [sb(f"y_{i}", [128, S]) for i in range(2)]

        fill = [pb(f"fill_{i}", [128, 512]) for i in range(FILL_BANKS)]
        turned = [pb(f"turned_{i}", [128, 512]) for i in range(PT_BANKS)]
        z_bank = pb("z_bank", [128, 512])
        misc = pb("misc", [128, 512])

        weights_loaded = sem("weights_loaded")
        x_loaded = [sem(f"x_loaded_{i}") for i in range(2)]
        c_loaded = [sem(f"c_loaded_{i}") for i in range(2)]
        x_res_loaded = [sem(f"x_res_loaded_{i}") for i in range(2)]
        y_free = [sem(f"y_free_{i}") for i in range(2)]
        consts_ready = sem("consts_ready")
        w_mm = sem("w_mm")
        w_dve = sem("w_dve")
        moments_ready = sem("moments_ready")
        mean_var_ready = sem("mean_var_ready")
        mean_summed = sem("mean_summed")
        centred_ready = sem("centred_ready")
        squared_ready = sem("squared_ready")
        spread_ready = sem("spread_ready")
        var_summed = sem("var_summed")
        variance_ready = sem("variance_ready")
        rstd_ready = sem("rstd_ready")
        xhat_ready = sem("xhat_ready")
        x_hi_ready = sem("x_hi_ready")
        x_stack_ready = sem("x_stack_ready")
        c_hi_ready = sem("c_hi_ready")
        c_lo_ready = sem("c_lo_ready")
        ctx_turned = sem("ctx_turned")
        ctx_t_ready = sem("ctx_t_ready")
        projected = sem("projected")
        t_hi_ready = sem("t_hi_ready")
        t_lo_ready = sem("t_lo_ready")
        scored = sem("scored")
        max_ready = sem("max_ready")
        exp_ready = sem("exp_ready")
        recip_ready = sem("recip_ready")
        probs_ready = sem("probs_ready")
        probs_turned = sem("probs_turned")
        probs_t_act = sem("probs_t_act")
        probs_t_dve = sem("probs_t_dve")
        z_summed = sem("z_summed")
        z_ready = sem("z_ready")
        out_summed = sem("out_summed")
        y_ready = sem("y_ready")

        ACT_EVACS = [u for u in range(UNITS) if u not in DVE_EVACS]

        def probs_t_wait(eng, pair, unit):
            if unit in DVE_EVACS:
                order = sorted(DVE_EVACS)
                wait(eng, probs_t_dve, pair.count(len(order), order.index(unit) + 1))
            else:
                wait(eng, probs_t_act, pair.count(len(ACT_EVACS), ACT_EVACS.index(unit) + 1))

        N_WEIGHT_DMAS = 14
        block = stack.enter_context(nc.Block())

        @block.sync
        def _(sync):
            def load_x(pair, row):
                p = pair.parity()
                src = x[bass.ds(row, PS), :, :].rearrange("s c q -> c s q")
                for half in range(2):
                    sync.dma_start(x2[p][64 * half:64 * half + 64, :, :], src).then_inc(x_loaded[p], 16)

            def load_c(pair, row):
                p = pair.parity()
                src = ctx[bass.ds(row, PS), :, :].rearrange("s c q -> c s q")
                for half in range(2):
                    sync.dma_start(c2[p][64 * half:64 * half + 64, :, :], src).then_inc(c_loaded[p], 16)

            load_x(Pair(0, 0), 0)
            for p in range(2):
                sync.sem_inc(y_free[p], 16)
            sync.wait_ge(consts_ready, 1)
            for dst, src in (
                [(wq2[:, :, i, :], Wq.rearrange("(p r) c -> r p c", r=128)) for i in range(2)]
                + [(wk2[:, :, i, :], Wkv[0:H * C, :].rearrange("(p r) c -> r p c", r=128)) for i in range(2)]
                + [(wv[:, :, :], Wkv[H * C:2 * H * C, :].rearrange("(p r) c -> r p c", r=128)),
                   (wo[:, :], Wo),
                   (bq_cols[0:64, :, 0], bq.rearrange("(p r) -> r p", r=128)[0:64, :]),
                   (bq_cols[64:128, :, 1], bq.rearrange("(p r) -> r p", r=128)[64:128, :]),
                   (bv_col[:, :], bkv[H * C:2 * H * C].rearrange("(p r) -> r p", r=128)),
                   (beta_col[:, :], beta.unsqueeze(1)),
                   (gamma2[0:64, :], gamma.unsqueeze(1)),
                   (gamma2[64:128, :], gamma.unsqueeze(1)),
                   (bo2[0:64, :], bo.unsqueeze(1)),
                   (bo2[64:128, :], bo.unsqueeze(1))]
            ):
                sync.dma_start(dst, src, allow_slow_non_contiguous=True).then_inc(weights_loaded, 16)
            load_c(Pair(0, 0), 0)
            load_x(Pair(0, 1), 2)
            load_c(Pair(0, 1), 2)

            def steps(pair):
                nxt, prev = pair.shift(2), pair.shift(-1)
                p = pair.parity()
                row, nxt_row, prev_row = (q.rows() if isinstance(q.j, int) else sync.snap(q.rows())
                                          for q in (pair, nxt, prev))
                if nxt.exists():
                    wait(sync, xhat_ready, pair.count(2, 2))
                    load_x(nxt, nxt_row)
                    wait(sync, c_lo_ready, pair.count(2, 2))
                    wait(sync, ctx_turned, pair.count(2, 2))
                    load_c(nxt, nxt_row)
                if pair.exists():
                    wait(sync, ctx_t_ready, pair.count(1, 1))
                    sync.dma_start(x_res[p][:, :], x[bass.ds(row, PS), :, :].rearrange("s c q -> (s c) q")
                                   ).then_inc(x_res_loaded[p], 16)
                if prev.exists():
                    wait(sync, y_ready, prev.count(1, 1))
                    sync.dma_start(out[bass.ds(prev_row, PS), :, :].rearrange("s c q -> (s c) q"),
                                   y[prev.parity()][:, :]).then_inc(y_free[prev.parity()], 16)

            steps(Pair(0, 0))
            with sync.Fori(0, (NPAIR - 4) // 2) as j:
                steps(Pair(j, 1))
                steps(Pair(j, 2))
            for c in range(NPAIR - 3, NPAIR + 1):
                steps(Pair(0, c))
            for p in range(2):
                sync.wait_ge(y_free[p], 16 * (NPAIR // 2 + 1))

        @block.tensor
        def _(pe):
            def weight_products():
                pe.wait_ge(weights_loaded, 16 * N_WEIGHT_DMAS)
                pe.wait_ge(consts_ready, 5)
                for h in range(H):
                    r = 64 * (h % 2)
                    mm = pe.matmul(fill[h % 2][:, 128 * (h // 2):128 * (h // 2) + 128],
                                   wq2[r:r + 64, h // 2, :, :], wk2[r:r + 64, h // 2, :, :],
                                   start=True, stop=True)
                mm.then_inc(w_mm, 1)
                for p in range(HP):
                    mm = pe.transpose(fill[2][:, 64 * p:64 * p + 64], wo[:, 128 * p:128 * p + 128], ident[0:64, 0:64])
                mm.then_inc(w_mm, 1)
                pe.wait_ge(w_dve, 2)
                for h in range(H):
                    pe.matmul(misc[:, h:h + 1], qk[:, h, :], beta_col[:, :], start=True, stop=True)
                for p in range(HP):
                    mm = pe.matmul(misc[:, H + 2 * p:H + 2 * p + 2], wk2[:, p, :, :], bq_cols[:, p, :],
                                   start=True, stop=True)
                mm.then_inc(w_mm, 1)
                pe.wait_ge(w_dve, 4)
                for p in range(HP):
                    for r in (0, 64):
                        mm = pe.matmul(fill[3][r:r + 64, 64 * p:64 * p + 64], wv[r:r + 64, p, :],
                                       wo_t2[r:r + 64, p, 0, :], start=True, stop=True)
                mm.then_inc(w_mm, 1)
                for p in range(HP):
                    mm = pe.matmul(z_bank[:, 0:1], wo_t2[:, p, :, :], bv_col[:, p:p + 1],
                                   start=(p == 0), stop=(p == HP - 1))
                mm.then_inc(w_mm, 1)
                pe.wait_ge(w_dve, W_DVE)

            def free_bank(pair, k):
                k -= FILL_BANKS
                if k < 0:
                    pair, k = pair.shift(-1), k + NFILL
                kind, item = FILLS[k]
                if kind == "scores":
                    owner, unit = of_step(pair, item)
                    if owner.exists():
                        wait(pe, exp_ready, owner.count(UNITS, unit + 1))
                elif pair.shift(1).exists():
                    wait(pe, t_lo_ready, pair.shift(1).count(H, item + 1))

            def scores(pair, unit, k):
                owner, v = of_step(pair, unit)
                if not owner.exists():
                    return
                h, s, p = v // PS, v % PS, owner.parity()
                if v == 0:
                    wait(pe, c_lo_ready, owner.count(2, 2))
                if s == 0:
                    wait(pe, t_lo_ready, owner.count(H, h + 1))
                free_bank(pair, k)
                bank = fill[k % FILL_BANKS]
                for qt in range(QT):
                    lhs = t_stack[:, h, s, 128 * qt:128 * qt + 128]
                    dst = bank[:, K * qt:K * qt + K]
                    pe.matmul(dst, lhs, c_straight[p][:, s, :], start=True, stop=False)
                    mm = pe.matmul(dst, lhs, c_crossed[p][:, s, :], start=False, stop=True)
                mm.then_inc(scored, 1)

            def project(pair, h, k):
                owner = pair.shift(1)
                if not owner.exists():
                    return
                if h == 0:
                    wait(pe, x_stack_ready, owner.count(1, 1))
                free_bank(pair, k)
                bank = fill[k % FILL_BANKS]
                pe.matmul(bank[:, :], w_straight[:, h, :], x_stack[:, :, :], start=True, stop=False)
                pe.matmul(bank[:, :], w_crossed[:, h, :], x_stack[:, :, :], start=False, stop=True
                          ).then_inc(projected, 1)

            def turn_probs(pair, unit):
                wait(pe, probs_ready, pair.count(UNITS, unit + 1))
                owner, v = of_step(pair, unit - PT_BANKS)
                if owner.exists():
                    probs_t_wait(pe, owner, v)
                for kt in range(KT):
                    for qt in range(QT):
                        mm = pe.transpose(turned[unit % PT_BANKS][:, S * kt + 128 * qt:S * kt + 128 * qt + 128],
                                          probs[:, unit % PROBS, qt, 128 * kt:128 * kt + 128], ident[:, :])
                mm.then_inc(probs_turned, 1)

            def times_context(pair, hp, s):
                units = [2 * PS * hp + s, 2 * PS * hp + PS + s]
                for unit in units:
                    probs_t_wait(pe, pair, unit)
                if s == 0:
                    wait(pe, z_ready, pair.count(HP, hp))
                    if hp == 0:
                        wait(pe, ctx_t_ready, pair.count(1, 1))
                for kt in range(KT):
                    for half in range(2):
                        mm = pe.matmul(z_bank[64 * half:64 * half + 64, S * s:S * s + S],
                                       ctx_t[pair.parity()][:, s, kt, :],
                                       probs_t[:, units[half] % PROBS_T, kt, :],
                                       start=(kt == 0), stop=(kt == KT - 1))
                if s == PS - 1:
                    mm.then_inc(z_summed, 1)

            def project_out(pair):
                wait(pe, z_ready, pair.count(HP, HP))
                if pair.shift(2).exists():
                    wait(pe, variance_ready, pair.shift(2).count(1, 1))
                for hp in range(HP):
                    for s in range(PS):
                        mm = pe.matmul(misc[64 * s:64 * s + 64, 0:S], u_t[:, hp, :], z[:, hp, s, :],
                                       start=(hp == 0), stop=(hp == HP - 1))
                mm.then_inc(out_summed, 1)

            def turn_context(pair):
                wait(pe, c_loaded[pair.parity()], pair.dma_count(1) * 2)
                wait(pe, y_ready, pair.count(1, -1))
                if not isinstance(pair.j, int) or pair.c < 2:
                    wait(pe, variance_ready, pair.count(1, 1))
                for s in range(PS):
                    for kt in range(KT):
                        at = 128 * (KT * s + kt)
                        mm = pe.transpose(misc[:, at:at + 128], c2[pair.parity()][:, s, 128 * kt:128 * kt + 128],
                                          ident[:, :])
                    mm.then_inc(ctx_turned, 1)

            def steps(pair):
                nxt = pair.shift(1)
                for u in range(UNITS):
                    k = FILLS.index(("scores", u + LEAD))
                    scores(pair, u + LEAD, k)
                    if nxt.exists() and u == MEAN_STEP:
                        wait(pe, mean_var_ready, nxt.count(2, 2))
                        wait(pe, ctx_t_ready, nxt.count(1, 0))
                        pe.matmul(misc[:, 0:PS], ones[:, :], mean_var[:, :, 0], start=True, stop=True
                                  ).then_inc(mean_summed, 1)
                    if nxt.exists() and u == VAR_STEP:
                        wait(pe, spread_ready, nxt.count(1, 1))
                        pe.matmul(misc[:, PS:2 * PS], ones[:, :], spread[:, :], start=True, stop=True
                                  ).then_inc(var_summed, 1)
                    if u in PROJ_STEP:
                        project(pair, PROJ_STEP.index(u), k + 1)
                    if pair.exists():
                        turn_probs(pair, u)
                    for hp in range(HP):
                        for s in range(PS):
                            ahead = 2 * PS * (hp + 1) + s - u
                            if ahead % UNITS == 0 and pair.shift(-(ahead != 0)).exists():
                                times_context(pair.shift(-(ahead != 0)), hp, s)
                    if u == OUT_STEP % UNITS and pair.shift(-1).exists():
                        project_out(pair.shift(-1))
                    if u == CTX_T_STEP and nxt.exists():
                        turn_context(nxt)

            weight_products()
            walk(pe, steps)

        @block.scalar
        def _(act):
            def copy_turned(pair, unit):
                wait(act, probs_turned, pair.count(UNITS, unit + 1))
                hp = unit // (2 * PS)
                owner, older = of_step(pair, 2 * PS * hp - PROBS_T)
                if owner.exists():
                    wait(act, z_summed, owner.count(HP, older // (2 * PS) + 1))
                act.copy(probs_t[:, unit % PROBS_T, :, :], turned[unit % PT_BANKS][:, :]
                         ).then_inc(probs_t_act, 1)

            def exponentials(pair, unit):
                bank = fill[bank_of_unit(unit)]
                wait(act, max_ready, pair.count(UNITS, unit + 1))
                wait(act, probs_turned, pair.count(UNITS, unit + 1 - PROBS))
                for qt in range(QT):
                    ins = act.activation(probs[:, unit % PROBS, qt, :], bank[:, K * qt:K * qt + K], ACT.Exp,
                                         bias=neg_max[:, unit, qt:qt + 1], accum_out=denom[:, unit, qt:qt + 1])
                ins.then_inc(exp_ready, 1)

            def t_hi(pair, h):
                wait(act, projected, pair.count(H, h + 1))
                act.activation(t_stack[:, h, :, :], fill[bank_of("proj", h)][:, :], ACT.Identity,
                               bias=d_col[:, h:h + 1]).then_inc(t_hi_ready, 1)

            def copy_z(pair, hp):
                wait(act, z_summed, pair.count(HP, hp + 1))
                if hp == 0:
                    wait(act, out_summed, pair.count(1, 0))
                act.copy(z[:, hp, :, :], z_bank[:, :]).then_inc(z_ready, 1)

            def steps(pair):
                nxt = pair.shift(1)
                for u in range(UNITS):
                    owner, v = of_step(pair, u - 1)
                    if owner.exists() and v not in DVE_EVACS:
                        copy_turned(owner, v)
                    for hp in range(HP):
                        ahead = 2 * PS * (hp + 1) + 2 - u
                        if ahead % UNITS == 0 and pair.shift(-(ahead != 0)).exists():
                            copy_z(pair.shift(-(ahead != 0)), hp)
                    owner, v = of_step(pair, u + LEAD)
                    if owner.exists():
                        exponentials(owner, v)
                    if u in PROJ_STEP and nxt.exists():
                        t_hi(nxt, PROJ_STEP.index(u))

            act.wait_ge(w_dve, W_DVE)
            walk(act, steps)

        @block.vector
        def _(dve):
            def weights():
                dve.wait_ge(weights_loaded, 16 * N_WEIGHT_DMAS)
                dve.tensor_scalar(gamma_scaled[:, :], gamma2[:, :], SCALE, None, ALU.mult).then_inc(w_dve, 1)
                dve.wait_ge(w_mm, 1)
                for i in range(2):
                    ins = dve.tensor_copy(qk[:, i::2, :], fill[i][0:64, :].rearrange("r (p c) -> r p c", p=HP))
                ins.then_inc(w_dve, 1)
                dve.wait_ge(w_mm, 2)
                for i in range(2):
                    dve.tensor_copy(wo_t2[:, :, i, :], fill[2][:, 0:256]).then_inc(w_dve, 1)
                dve.wait_ge(w_dve, 1)
                for i in range(2):
                    dve.tensor_scalar(qk_gamma[:, i::2, :], fill[i][:, :].rearrange("r (p c) -> r p c", p=HP),
                                      gamma_scaled[:, 0:1], None, ALU.mult).then_inc(w_dve, 1)
                dve.wait_ge(w_dve, 6)
                dve.tensor_copy(w_straight[:, :, :], qk_gamma[:, :, :]).then_inc(w_dve, 1)
                dve.tensor_copy(w_crossed[:, :, :], qk_gamma[:, :, :]).then_inc(w_dve, 1)
                dve.wait_ge(w_dve, 8)
                for w, r in ((w_straight, 64), (w_crossed, 0)):
                    dve.tensor_tensor(w[r:r + 64, :, :], qk_gamma[r:r + 64, :, :], w[r:r + 64, :, :].bitcast(F32),
                                      ALU.subtract).then_inc(w_dve, 1)
                dve.wait_ge(w_mm, 3)
                dve.tensor_scalar(d_part[:, :], misc[:, 0:H], SCALE, None, ALU.mult).then_inc(w_dve, 1)
                dve.wait_ge(w_dve, 11)
                dve.scalar_tensor_tensor(out=d_col[:, :], in0=misc[:, H:2 * H], scalar=SCALE, in1=d_part[:, :],
                                         op0=ALU.mult, op1=ALU.add).then_inc(w_dve, 1)
                dve.wait_ge(w_mm, 4)
                dve.tensor_copy(u_t[:, :, :], fill[3][:, 0:256]).then_inc(w_dve, 1)
                dve.wait_ge(w_mm, 5)
                dve.tensor_tensor(out_bias[:, :], z_bank[:, 0:1], bo2[:, :], ALU.add).then_inc(w_dve, 1)

            def copy_turned(pair, unit):
                wait(dve, probs_turned, pair.count(UNITS, unit + 1))
                hp = unit // (2 * PS)
                owner, older = of_step(pair, 2 * PS * hp - PROBS_T)
                if owner.exists():
                    wait(dve, z_summed, owner.count(HP, older // (2 * PS) + 1))
                dve.tensor_copy(probs_t[:, unit % PROBS_T, :, :], turned[unit % PT_BANKS][:, :]
                                ).then_inc(probs_t_dve, 1)

            def row_max(pair, unit):
                wait(dve, scored, pair.count(UNITS, unit + 1))
                dve.tensor_reduce(neg_max[:, unit, :],
                                  fill[bank_of_unit(unit)][:, :].rearrange("p (t k) -> p t k", t=QT),
                                  AX.X, ALU.max, negate=True).then_inc(max_ready, 1)

            def reciprocal(pair, unit):
                wait(dve, exp_ready, pair.count(UNITS, unit + 1))
                dve.reciprocal(recip[:, unit, :], denom[:, unit, :]).then_inc(recip_ready, 1)

            def t_lo(pair, h):
                wait(dve, t_hi_ready, pair.count(H, h + 1))
                half = t_stack[64:128, h, :, :]
                dve.scalar_tensor_tensor(out=half, in0=fill[bank_of("proj", h)][64:128, :], scalar=d_col[64:128, h:h + 1],
                                         in1=half.bitcast(F32), op0=ALU.add, op1=ALU.subtract
                                         ).then_inc(t_lo_ready, 1)

            def channel_moments(pair):
                p = pair.parity()
                wait(dve, x_loaded[p], pair.dma_count(1) * 2)
                for s in range(PS):
                    dve.bn_stats(moments[:, s, :], x2[p][:, s, :]).then_inc(moments_ready, 1)

            def channel_mean_var(pair):
                for s in range(PS):
                    dve.bn_aggr(mean_var[:, s, :], moments[:, s, :]).then_inc(mean_var_ready, 1)

            def channel_spread(pair):
                wait(dve, mean_summed, pair.count(1, 1))
                dve.tensor_copy(mean[:, :], misc[:, 0:PS]).then_inc(centred_ready, 1)
                dve.tensor_tensor(centred[:, :], mean_var[:, :, 0], misc[:, 0:PS], ALU.subtract
                                  ).then_inc(centred_ready, 1)
                wait(dve, centred_ready, pair.count(2, 2))
                dve.tensor_tensor(squared[:, :], centred[:, :], centred[:, :], ALU.mult).then_inc(squared_ready, 1)
                wait(dve, squared_ready, pair.count(1, 1))
                dve.tensor_tensor(spread[:, :], squared[:, :], mean_var[:, :, 1], ALU.add).then_inc(spread_ready, 1)

            def sample_variance(pair):
                wait(dve, var_summed, pair.count(1, 1))
                dve.tensor_scalar(variance[:, :], misc[:, PS:2 * PS], EPS, None, ALU.add).then_inc(variance_ready, 1)

            def normalise(pair):
                wait(dve, rstd_ready, pair.count(1, 1))
                wait(dve, projected, pair.count(H, 0))
                for s in range(PS):
                    dve.tensor_scalar(xhat[:, s, :], x2[pair.parity()][:, s, :], mean[:, s:s + 1], rstd[:, s:s + 1],
                                      ALU.subtract, ALU.mult).then_inc(xhat_ready, 1)
                wait(dve, xhat_ready, pair.count(2, 2))
                dve.tensor_copy(x_stack[:, :, :], xhat[:, :, :]).then_inc(x_hi_ready, 1)

            def context_hi(pair):
                p = pair.parity()
                wait(dve, c_loaded[p], pair.dma_count(1) * 2)
                dve.tensor_copy(c_straight[p][0:64, :, :], c2[p][0:64, :, :]).then_inc(c_hi_ready, 1)
                dve.tensor_copy(c_crossed[p][64:128, :, :], c2[p][64:128, :, :]).then_inc(c_hi_ready, 1)

            def copy_ctx_t(pair):
                wait(dve, ctx_turned, pair.count(2, 2))
                wait(dve, z_summed, pair.count(HP, -HP))
                dve.tensor_copy(ctx_t[pair.parity()][:, :, :, :].rearrange("p s t c -> p (s t) c"),
                                misc[:, :].rearrange("p (n c) -> p n c", c=2 * CK)[:, :, 0:CK]
                                ).then_inc(ctx_t_ready, 1)

            def result(pair):
                p = pair.parity()
                wait(dve, out_summed, pair.count(1, 1))
                wait(dve, x_res_loaded[p], pair.dma_count(1))
                wait(dve, y_free[p], pair.dma_count(1))
                dve.scalar_tensor_tensor(out=y[p][:, :], in0=misc[:, 0:S], scalar=out_bias[:, 0:1], in1=x_res[p][:, :],
                                         op0=ALU.add, op1=ALU.add).then_inc(y_ready, 1)

            def steps(pair):
                nxt = pair.shift(1)
                for u in range(UNITS):
                    owner, v = of_step(pair, u - 1)
                    if owner.exists() and v in DVE_EVACS:
                        copy_turned(owner, v)
                    if nxt.exists() and u == MEAN_STEP - 1:
                        wait(dve, moments_ready, nxt.count(2, 2))
                    owner, v = of_step(pair, u + LEAD)
                    if owner.exists():
                        row_max(owner, v)
                    owner, v = of_step(pair, u + LEAD - 1)
                    if owner.exists() and not (isinstance(owner.j, int) and owner.c == 0 and v < 0):
                        reciprocal(owner, v)
                    if u in PROJ_STEP and nxt.exists():
                        t_lo(nxt, PROJ_STEP.index(u))
                    if nxt.exists():
                        if u == MEAN_STEP - 2:
                            channel_moments(nxt)
                        if u == MEAN_STEP - 1:
                            channel_mean_var(nxt)
                        if u == MEAN_STEP:
                            channel_spread(nxt)
                        if u == VAR_STEP:
                            sample_variance(nxt)
                        if u == VAR_STEP + 1:
                            normalise(nxt)
                        if u == 7:
                            context_hi(nxt)
                        if u == CTX_T_STEP + 1:
                            copy_ctx_t(nxt)
                    if u == OUT_STEP % UNITS and pair.shift(-1).exists():
                        result(pair.shift(-1))

            weights()
            walk(dve, steps)

        @block.gpsimd
        def _(pool):
            pool.memset(bq_cols[:, :, :], 0.0).then_inc(consts_ready, 1)
            pool.memset(ident[:, :], 0.0).then_inc(consts_ready, 1)
            pool.memset(ones[:, :], 1.0 / 128).then_inc(consts_ready, 1)
            pool.memset(minus_half[:, :], -0.5).then_inc(consts_ready, 1)
            pool.wait_ge(consts_ready, 4)
            pool.affine_select(out=ident[:, :], in_=ident[:, :], compare_op=ALU.not_equal, fill=1.0, base=0,
                               pattern=[[-1, 128]], channel_multiplier=1).then_inc(consts_ready, 1)

            def divide(pair, unit):
                wait(pool, recip_ready, pair.count(UNITS, unit + 1))
                p = probs[:, unit % PROBS, :, :]
                pool.tensor_tensor(p, p, recip[:, unit, :].unsqueeze(2).broadcast_to([128, QT, K]), ALU.mult
                                   ).then_inc(probs_ready, 1)

            def inverse_root(pair):
                wait(pool, variance_ready, pair.count(1, 1))
                pool.tensor_tensor(rstd[:, :], variance[:, :], minus_half[:, :], ALU.pow).then_inc(rstd_ready, 1)

            def x_lo(pair):
                wait(pool, x_hi_ready, pair.count(1, 1))
                half = x_stack[64:128, :, :]
                pool.tensor_tensor(half, xhat[64:128, :, :], half.bitcast(F32), ALU.subtract).then_inc(x_stack_ready, 1)

            def context_lo(pair):
                p = pair.parity()
                wait(pool, c_hi_ready, pair.count(2, 2))
                pool.tensor_tensor(c_straight[p][64:128, :, :], c2[p][64:128, :, :],
                                   c_crossed[p][64:128, :, :].bitcast(F32), ALU.subtract).then_inc(c_lo_ready, 1)
                wait(pool, c_lo_ready, pair.count(2, 1))
                pool.tensor_tensor(c_crossed[p][0:64, :, :], c2[p][0:64, :, :],
                                   c_straight[p][0:64, :, :].bitcast(F32), ALU.subtract).then_inc(c_lo_ready, 1)

            def steps(pair):
                nxt = pair.shift(1)
                for u in range(UNITS):
                    owner, v = of_step(pair, u + LEAD - 1)
                    if owner.exists():
                        divide(owner, v)
                    if nxt.exists():
                        if u == VAR_STEP:
                            inverse_root(nxt)
                        if u in (VAR_STEP + 1, 8) and owner.exists():
                            wait(pool, probs_ready, owner.count(UNITS, v + 1))
                        if u == VAR_STEP + 1:
                            x_lo(nxt)
                            wait(pool, x_stack_ready, nxt.count(1, 1))
                        if u == 8:
                            context_lo(nxt)
                            wait(pool, c_lo_ready, nxt.count(2, 2))

            walk(pool, steps)


W_DVE = 14


def bank_of_unit(unit):
    return bank_of("scores", unit if unit >= LEAD else unit + UNITS)


_INS = ["x", "ctx_2048", "L0_xattn_gamma", "L0_xattn_beta", "L0_xattn_Wq", "L0_xattn_bq", "L0_xattn_Wkv",
        "L0_xattn_bkv", "L0_xattn_Wo", "L0_xattn_bo"]


def kernel(**inputs):
    import numpy as np
    import concourse.bacc as bacc
    from concourse.bass_utils import run_bass_kernel_spmd

    nc = bacc.Bacc("TRN2", target_bir_lowering=False, num_devices=1)
    arrays, args = {}, []
    for name in _INS:
        a = np.ascontiguousarray(inputs[name])
        arrays[f"in_{name}"] = a
        args.append(nc.dram_tensor(f"in_{name}", a.shape, mybir.dt.from_np(a.dtype), kind="ExternalInput").ap())
    args.append(nc.dram_tensor("out", (B, C, S), F32, kind="ExternalOutput").ap())
    build(nc, *args)
    r = run_bass_kernel_spmd(nc, [arrays], core_ids=[0])
    return r.results[0]["out"]
```

```python
from contextlib import ExitStack

import concourse.bass as bass
from concourse import mybir

F32 = mybir.dt.float32
F32R = mybir.dt.float32r
ALU = mybir.AluOpType
ACT = mybir.ActivationFunctionType
AX = mybir.AxisListType

B, C, S = 64, 64, 256
K, CK = 256, 64
H = 8
EPS = 1e-5
SCALE = float(C) ** -0.5

PS = 2
NPAIR = B // PS
UNITS = PS * H
QT = S // 128
KT = K // 128
HP = H // 2

LEAD = 4
FILL_BANKS = 4
PT_BANKS = 2
PROBS = 8
PROBS_T = 8

PROJ_STEP = [2 * _h - 9 for _h in range(H)]
T_HI_STEP = [_s + 1 for _s in PROJ_STEP]
T_LO_STEP = [_s + 1 for _s in PROJ_STEP]
TIMES_CTX_STEP = {(_hp, _s): 4 * _hp + 4 + 2 * _s for _hp in range(HP) for _s in range(PS)}
Z_STEP = [4 * _hp + 7 for _hp in range(HP)]
OUT_STEP = [UNITS + 5 + 2 * _hp for _hp in range(HP)]
RESULT_STEP = OUT_STEP[-1] + 1
MOMENTS_STEP, MEAN_STEP, SPREAD_STEP, VAR_STEP = -16, -15, -14, -14
RSTD_STEP, XHAT_STEP, X_LO_STEP = -13, -12, -11
C_HI_STEP, C_LO_STEP = -8, -7
CTX_T_STEP, CTX_COPY_STEP = -2, -1
DVE_EVACS = frozenset(range(0, UNITS, 2))

FILLS = []
for _u in range(UNITS):
    FILLS.append(("scores", (_u + LEAD) % UNITS, _u if _u + LEAD < UNITS else _u - UNITS))
    FILLS += [("proj", _h, PROJ_STEP[_h]) for _h in range(H) if PROJ_STEP[_h] % UNITS == _u]
NFILL = len(FILLS)
assert NFILL % FILL_BANKS == 0


def fill_of(kind, item):
    return [f[:2] for f in FILLS].index((kind, item))


def bank_of(kind, item):
    return fill_of(kind, item) % FILL_BANKS


class Pair:

    def __init__(self, j, c):
        self.j, self.c = j, c

    def shift(self, n):
        return Pair(self.j, self.c + n)

    def exists(self):
        return not isinstance(self.j, int) or 0 <= self.c < NPAIR

    def parity(self):
        return self.c % 2

    def count(self, per_pair, k):
        return self.j * (2 * per_pair) + (per_pair * self.c + k)

    def dma_count(self, k):
        return self.j * 16 + 16 * (self.c // 2 + k)

    def rows(self):
        return self.j * (2 * PS) + PS * self.c


def of_step(pair, item):
    return (pair.shift(item // UNITS), item % UNITS)


def due(pair, u, step):
    if step % UNITS != u:
        return None
    owner = pair.shift(-(step // UNITS))
    return owner if owner.exists() else None


def wait(eng, sem, value):
    if not isinstance(value, int) or value > 0:
        eng.wait_ge(sem, value)


def walk(eng, steps):
    steps(Pair(0, -1))
    steps(Pair(0, 0))
    with eng.Fori(0, (NPAIR - 2) // 2) as j:
        steps(Pair(j, 1))
        steps(Pair(j, 2))
    steps(Pair(0, NPAIR - 1))
    steps(Pair(0, NPAIR))


def build(nc, x, ctx, gamma, beta, Wq, bq, Wkv, bkv, Wo, bo, out):
    stack = ExitStack()
    with stack:
        def sb(name, shape, dt=F32):
            return stack.enter_context(nc.sbuf_tensor(name, shape, dt))

        def pb(name, shape):
            return stack.enter_context(nc.psum_tensor(name, shape, F32))

        def sem(name):
            return stack.enter_context(nc.semaphore(name))

        wq2 = sb("wq2", [128, HP, 2, C])
        wk2 = sb("wk2", [128, HP, 2, CK])
        wv = sb("wv", [128, HP, CK])
        wo = sb("wo", [C, H * C])
        bq_cols = sb("bq_cols", [128, HP, 2])
        bv_col = sb("bv_col", [128, HP])
        bo2 = sb("bo2", [128, 1])
        gamma2 = sb("gamma2", [128, 1])
        beta_col = sb("beta_col", [C, 1])
        gamma_scaled = sb("gamma_scaled", [128, 1])
        qk = sb("qk", [C, H, 2 * CK])
        qk_gamma = sb("qk_gamma", [128, H, 2 * CK])
        w_straight = sb("w_straight", [128, H, 2 * CK], F32R)
        w_crossed = sb("w_crossed", [128, H, 2 * CK], F32R)
        d_part = sb("d_part", [128, H])
        d_col = sb("d_col", [128, H])
        wo_t2 = sb("wo_t2", [128, HP, 2, C])
        u_t = sb("u_t", [128, HP, C])
        out_bias = sb("out_bias", [128, 1])
        ident = sb("ident", [128, 128])
        ones = sb("ones", [128, 128])
        minus_half = sb("minus_half", [128, PS])
        x2 = [sb(f"x2_{i}", [128, PS, S]) for i in range(2)]
        c2 = [sb(f"c2_{i}", [128, PS, K]) for i in range(2)]
        x_res = [sb(f"x_res_{i}", [128, S]) for i in range(2)]
        moments = sb("moments", [128, PS, 6])
        mean_var = sb("mean_var", [128, PS, 2])
        mean = sb("mean", [128, PS])
        centred = sb("centred", [128, PS])
        squared = sb("squared", [128, PS])
        spread = sb("spread", [128, PS])
        variance = sb("variance", [128, PS])
        rstd = sb("rstd", [128, PS])
        xhat = [sb(f"xhat_{i}", [128, PS, S]) for i in range(2)]
        x_stack = [sb(f"x_stack_{i}", [128, PS, S], F32R) for i in range(2)]
        c_straight = [sb(f"c_straight_{i}", [128, PS, K], F32R) for i in range(2)]
        c_crossed = [sb(f"c_crossed_{i}", [128, PS, K], F32R) for i in range(2)]
        ctx_t = [sb(f"ctx_t_{i}", [128, PS, KT, CK]) for i in range(2)]
        t_stack = sb("t_stack", [128, H, PS, S], F32R)
        neg_max = sb("neg_max", [128, UNITS, QT])
        denom = sb("denom", [128, UNITS, QT])
        recip = sb("recip", [128, UNITS, QT])
        probs = sb("probs", [128, PROBS, QT, K])
        probs_t = sb("probs_t", [128, PROBS_T, KT, S])
        z = [sb(f"z_{i}", [128, HP, PS, S]) for i in range(2)]
        y = [sb(f"y_{i}", [128, S]) for i in range(2)]

        fill = [pb(f"fill_{i}", [128, 512]) for i in range(FILL_BANKS)]
        turned = [pb(f"turned_{i}", [128, 512]) for i in range(PT_BANKS)]
        z_bank = pb("z_bank", [128, 512])
        misc = pb("misc", [128, 512])

        weights_loaded = sem("weights_loaded")
        x_loaded = [sem(f"x_loaded_{i}") for i in range(2)]
        c_loaded = [sem(f"c_loaded_{i}") for i in range(2)]
        x_res_loaded = [sem(f"x_res_loaded_{i}") for i in range(2)]
        y_free = [sem(f"y_free_{i}") for i in range(2)]
        consts_ready = sem("consts_ready")
        w_mm = sem("w_mm")
        w_dve = sem("w_dve")
        moments_ready = sem("moments_ready")
        mean_var_ready = sem("mean_var_ready")
        mean_summed = sem("mean_summed")
        centred_ready = sem("centred_ready")
        squared_ready = sem("squared_ready")
        spread_ready = sem("spread_ready")
        var_summed = sem("var_summed")
        variance_ready = sem("variance_ready")
        rstd_ready = sem("rstd_ready")
        xhat_ready = sem("xhat_ready")
        x_hi_ready = sem("x_hi_ready")
        x_stack_ready = sem("x_stack_ready")
        c_hi_ready = sem("c_hi_ready")
        c_lo_ready = sem("c_lo_ready")
        ctx_turned = sem("ctx_turned")
        ctx_t_ready = sem("ctx_t_ready")
        projected = sem("projected")
        t_hi_ready = sem("t_hi_ready")
        t_lo_ready = sem("t_lo_ready")
        scored = sem("scored")
        max_ready = sem("max_ready")
        exp_ready = sem("exp_ready")
        recip_ready = sem("recip_ready")
        probs_ready = sem("probs_ready")
        probs_turned = sem("probs_turned")
        probs_t_act = sem("probs_t_act")
        probs_t_dve = sem("probs_t_dve")
        z_summed = sem("z_summed")
        z_ready = sem("z_ready")
        out_summed = sem("out_summed")
        y_ready = sem("y_ready")

        ACT_EVACS = [u for u in range(UNITS) if u not in DVE_EVACS]

        def probs_t_wait(eng, pair, unit):
            if unit in DVE_EVACS:
                order = sorted(DVE_EVACS)
                wait(eng, probs_t_dve, pair.count(len(order), order.index(unit) + 1))
            else:
                wait(eng, probs_t_act, pair.count(len(ACT_EVACS), ACT_EVACS.index(unit) + 1))

        N_WEIGHT_DMAS = 14
        block = stack.enter_context(nc.Block())

        @block.sync
        def _(sync):
            def load_x(pair, row):
                p = pair.parity()
                src = x[bass.ds(row, PS), :, :].rearrange("s c q -> c s q")
                for half in range(2):
                    sync.dma_start(x2[p][64 * half:64 * half + 64, :, :], src).then_inc(x_loaded[p], 16)

            def load_c(pair, row):
                p = pair.parity()
                src = ctx[bass.ds(row, PS), :, :].rearrange("s c q -> c s q")
                for half in range(2):
                    sync.dma_start(c2[p][64 * half:64 * half + 64, :, :], src).then_inc(c_loaded[p], 16)

            load_x(Pair(0, 0), 0)
            for p in range(2):
                sync.sem_inc(y_free[p], 16)
            sync.wait_ge(consts_ready, 1)
            for dst, src in (
                [(wq2[:, :, i, :], Wq.rearrange("(p r) c -> r p c", r=128)) for i in range(2)]
                + [(wk2[:, :, i, :], Wkv[0:H * C, :].rearrange("(p r) c -> r p c", r=128)) for i in range(2)]
                + [(wv[:, :, :], Wkv[H * C:2 * H * C, :].rearrange("(p r) c -> r p c", r=128)),
                   (wo[:, :], Wo),
                   (bq_cols[0:64, :, 0], bq.rearrange("(p r) -> r p", r=128)[0:64, :]),
                   (bq_cols[64:128, :, 1], bq.rearrange("(p r) -> r p", r=128)[64:128, :]),
                   (bv_col[:, :], bkv[H * C:2 * H * C].rearrange("(p r) -> r p", r=128)),
                   (beta_col[:, :], beta.unsqueeze(1)),
                   (gamma2[0:64, :], gamma.unsqueeze(1)),
                   (gamma2[64:128, :], gamma.unsqueeze(1)),
                   (bo2[0:64, :], bo.unsqueeze(1)),
                   (bo2[64:128, :], bo.unsqueeze(1))]
            ):
                sync.dma_start(dst, src, allow_slow_non_contiguous=True).then_inc(weights_loaded, 16)
            load_c(Pair(0, 0), 0)
            load_x(Pair(0, 1), 2)
            load_c(Pair(0, 1), 2)

            def steps(pair):
                nxt, prev = pair.shift(2), pair.shift(-1)
                p = pair.parity()
                row, nxt_row, prev_row = (q.rows() if isinstance(q.j, int) else sync.snap(q.rows())
                                          for q in (pair, nxt, prev))
                if nxt.exists():
                    wait(sync, xhat_ready, pair.count(2, 2))
                    load_x(nxt, nxt_row)
                    wait(sync, c_lo_ready, pair.count(2, 2))
                    wait(sync, ctx_turned, pair.count(2, 2))
                    load_c(nxt, nxt_row)
                if pair.exists():
                    wait(sync, ctx_t_ready, pair.count(1, 1))
                    sync.dma_start(x_res[p][:, :], x[bass.ds(row, PS), :, :].rearrange("s c q -> (s c) q")
                                   ).then_inc(x_res_loaded[p], 16)
                if prev.exists():
                    wait(sync, y_ready, prev.count(1, 1))
                    sync.dma_start(out[bass.ds(prev_row, PS), :, :].rearrange("s c q -> (s c) q"),
                                   y[prev.parity()][:, :]).then_inc(y_free[prev.parity()], 16)

            steps(Pair(0, 0))
            with sync.Fori(0, (NPAIR - 4) // 2) as j:
                steps(Pair(j, 1))
                steps(Pair(j, 2))
            for c in range(NPAIR - 3, NPAIR + 1):
                steps(Pair(0, c))
            for p in range(2):
                sync.wait_ge(y_free[p], 16 * (NPAIR // 2 + 1))

        @block.tensor
        def _(pe):
            def weight_products():
                pe.wait_ge(weights_loaded, 16 * N_WEIGHT_DMAS)
                pe.wait_ge(consts_ready, 5)
                for h in range(H):
                    r = 64 * (h % 2)
                    mm = pe.matmul(fill[h % 2][:, 128 * (h // 2):128 * (h // 2) + 128],
                                   wq2[r:r + 64, h // 2, :, :], wk2[r:r + 64, h // 2, :, :],
                                   start=True, stop=True)
                mm.then_inc(w_mm, 1)
                for p in range(HP):
                    mm = pe.transpose(fill[2][:, 64 * p:64 * p + 64], wo[:, 128 * p:128 * p + 128], ident[0:64, 0:64])
                mm.then_inc(w_mm, 1)
                pe.wait_ge(w_dve, 2)
                for h in range(H):
                    pe.matmul(misc[:, h:h + 1], qk[:, h, :], beta_col[:, :], start=True, stop=True)
                for p in range(HP):
                    mm = pe.matmul(misc[:, H + 2 * p:H + 2 * p + 2], wk2[:, p, :, :], bq_cols[:, p, :],
                                   start=True, stop=True)
                mm.then_inc(w_mm, 1)
                pe.wait_ge(w_dve, 4)
                for p in range(HP):
                    for r in (0, 64):
                        mm = pe.matmul(fill[3][r:r + 64, 64 * p:64 * p + 64], wv[r:r + 64, p, :],
                                       wo_t2[r:r + 64, p, 0, :], start=True, stop=True)
                mm.then_inc(w_mm, 1)
                for p in range(HP):
                    mm = pe.matmul(z_bank[:, 0:1], wo_t2[:, p, :, :], bv_col[:, p:p + 1],
                                   start=(p == 0), stop=(p == HP - 1))
                mm.then_inc(w_mm, 1)
                pe.wait_ge(w_dve, W_DVE)

            def free_bank(pair, k):
                k -= FILL_BANKS
                if k < 0:
                    pair, k = pair.shift(-1), k + NFILL
                kind, item, step = FILLS[k]
                owner = pair.shift(-(step // UNITS))
                if owner.exists():
                    if kind == "scores":
                        wait(pe, exp_ready, owner.count(UNITS, item + 1))
                    else:
                        wait(pe, t_lo_ready, owner.count(H, item + 1))

            def scores(pair, v, bank):
                h, s, p = v // PS, v % PS, pair.parity()
                for qt in range(QT):
                    lhs = t_stack[:, h, s, 128 * qt:128 * qt + 128]
                    dst = bank[:, K * qt:K * qt + K]
                    pe.matmul(dst, lhs, c_straight[p][:, s, :], start=True, stop=False)
                    mm = pe.matmul(dst, lhs, c_crossed[p][:, s, :], start=False, stop=True)
                mm.then_inc(scored, 1)

            def project(pair, h, bank):
                xs = x_stack[pair.parity()][:, :, :]
                pe.matmul(bank[:, :], w_straight[:, h, :], xs, start=True, stop=False)
                pe.matmul(bank[:, :], w_crossed[:, h, :], xs, start=False, stop=True).then_inc(projected, 1)

            def fill_bank(pair, k):
                kind, item, step = FILLS[k]
                owner = pair.shift(-(step // UNITS))
                if not owner.exists():
                    return
                free_bank(pair, k)
                if kind == "scores":
                    if item == 0:
                        wait(pe, c_lo_ready, owner.count(2, 2))
                    if item % PS == 0:
                        wait(pe, t_lo_ready, owner.count(H, item // PS + 1))
                    scores(owner, item, fill[k % FILL_BANKS])
                else:
                    if item == 0:
                        wait(pe, x_stack_ready, owner.count(1, 1))
                    project(owner, item, fill[k % FILL_BANKS])

            def turn_probs(pair, unit):
                wait(pe, probs_ready, pair.count(UNITS, unit + 1))
                owner, v = of_step(pair, unit - PT_BANKS)
                if owner.exists():
                    probs_t_wait(pe, owner, v)
                for kt in range(KT):
                    for qt in range(QT):
                        mm = pe.transpose(turned[unit % PT_BANKS][:, S * kt + 128 * qt:S * kt + 128 * qt + 128],
                                          probs[:, unit % PROBS, qt, 128 * kt:128 * kt + 128], ident[:, :])
                mm.then_inc(probs_turned, 1)

            def times_context(pair, hp, s):
                units = [2 * PS * hp + s, 2 * PS * hp + PS + s]
                for unit in units:
                    probs_t_wait(pe, pair, unit)
                if s == 0:
                    wait(pe, z_ready, pair.count(HP, hp))
                    if hp == 0:
                        wait(pe, ctx_t_ready, pair.count(1, 1))
                for kt in range(KT):
                    for half in range(2):
                        mm = pe.matmul(z_bank[64 * half:64 * half + 64, S * s:S * s + S],
                                       ctx_t[pair.parity()][:, s, kt, :],
                                       probs_t[:, units[half] % PROBS_T, kt, :],
                                       start=(kt == 0), stop=(kt == KT - 1))
                if s == PS - 1:
                    mm.then_inc(z_summed, 1)

            def project_out(pair, hp):
                wait(pe, z_ready, pair.count(HP, hp + 1))
                if hp == 0 and pair.shift(2).exists():
                    wait(pe, variance_ready, pair.shift(2).count(1, 1))
                for s in range(PS):
                    mm = pe.matmul(misc[64 * s:64 * s + 64, 0:S], u_t[:, hp, :], z[pair.parity()][:, hp, s, :],
                                   start=(hp == 0), stop=(hp == HP - 1))
                if hp == HP - 1:
                    mm.then_inc(out_summed, 1)

            def sum_means(pair):
                wait(pe, mean_var_ready, pair.count(2, 2))
                wait(pe, ctx_t_ready, pair.count(1, 0))
                pe.matmul(misc[:, 0:PS], ones[:, :], mean_var[:, :, 0], start=True, stop=True
                          ).then_inc(mean_summed, 1)

            def sum_spreads(pair):
                wait(pe, spread_ready, pair.count(1, 1))
                pe.matmul(misc[:, PS:2 * PS], ones[:, :], spread[:, :], start=True, stop=True
                          ).then_inc(var_summed, 1)

            def turn_context(pair):
                wait(pe, c_loaded[pair.parity()], pair.dma_count(1) * 2)
                wait(pe, y_ready, pair.count(1, -1))
                if not isinstance(pair.j, int) or pair.c < 2:
                    wait(pe, variance_ready, pair.count(1, 1))
                for s in range(PS):
                    for kt in range(KT):
                        at = 128 * (KT * s + kt)
                        mm = pe.transpose(misc[:, at:at + 128], c2[pair.parity()][:, s, 128 * kt:128 * kt + 128],
                                          ident[:, :])
                    mm.then_inc(ctx_turned, 1)

            def steps(pair):
                k = 0
                for u in range(UNITS):
                    while k < NFILL and FILLS[k][2] % UNITS == u:
                        fill_bank(pair, k)
                        k += 1
                    if pair.exists():
                        turn_probs(pair, u)
                    for (hp, s), step in TIMES_CTX_STEP.items():
                        if owner := due(pair, u, step):
                            times_context(owner, hp, s)
                    for hp in range(HP):
                        if owner := due(pair, u, OUT_STEP[hp]):
                            project_out(owner, hp)
                    if owner := due(pair, u, MEAN_STEP):
                        sum_means(owner)
                    if owner := due(pair, u, VAR_STEP):
                        sum_spreads(owner)
                    if owner := due(pair, u, CTX_T_STEP):
                        turn_context(owner)

            weight_products()
            walk(pe, steps)

        @block.scalar
        def _(act):
            def copy_turned(pair, unit):
                wait(act, probs_turned, pair.count(UNITS, unit + 1))
                hp = unit // (2 * PS)
                owner, older = of_step(pair, 2 * PS * hp - PROBS_T)
                if owner.exists():
                    wait(act, z_summed, owner.count(HP, older // (2 * PS) + 1))
                act.copy(probs_t[:, unit % PROBS_T, :, :], turned[unit % PT_BANKS][:, :]
                         ).then_inc(probs_t_act, 1)

            def exponentials(pair, unit):
                bank = fill[bank_of("scores", unit)]
                wait(act, max_ready, pair.count(UNITS, unit + 1))
                wait(act, probs_turned, pair.count(UNITS, unit + 1 - PROBS))
                for qt in range(QT):
                    ins = act.activation(probs[:, unit % PROBS, qt, :], bank[:, K * qt:K * qt + K], ACT.Exp,
                                         bias=neg_max[:, unit, qt:qt + 1], accum_out=denom[:, unit, qt:qt + 1])
                ins.then_inc(exp_ready, 1)

            def t_hi(pair, h):
                wait(act, projected, pair.count(H, h + 1))
                act.activation(t_stack[:, h, :, :], fill[bank_of("proj", h)][:, :], ACT.Identity,
                               bias=d_col[:, h:h + 1]).then_inc(t_hi_ready, 1)

            def copy_z(pair, hp):
                wait(act, z_summed, pair.count(HP, hp + 1))
                if hp == 0 and (not isinstance(pair.j, int) or pair.c > 1):
                    wait(act, out_summed, pair.count(1, -1))
                act.copy(z[pair.parity()][:, hp, :, :], z_bank[:, :]).then_inc(z_ready, 1)

            def steps(pair):
                for u in range(UNITS):
                    for h in range(H):
                        if owner := due(pair, u, T_HI_STEP[h]):
                            t_hi(owner, h)
                    owner, v = of_step(pair, u + LEAD - 1)
                    if owner.exists():
                        exponentials(owner, v)
                    owner, v = of_step(pair, u - 1)
                    if owner.exists() and v not in DVE_EVACS:
                        copy_turned(owner, v)
                    for hp in range(HP):
                        if owner := due(pair, u, Z_STEP[hp]):
                            copy_z(owner, hp)

            act.wait_ge(w_dve, W_DVE)
            walk(act, steps)

        @block.vector
        def _(dve):
            def weights():
                dve.wait_ge(weights_loaded, 16 * N_WEIGHT_DMAS)
                dve.tensor_scalar(gamma_scaled[:, :], gamma2[:, :], SCALE, None, ALU.mult).then_inc(w_dve, 1)
                dve.wait_ge(w_mm, 1)
                for i in range(2):
                    ins = dve.tensor_copy(qk[:, i::2, :], fill[i][0:64, :].rearrange("r (p c) -> r p c", p=HP))
                ins.then_inc(w_dve, 1)
                dve.wait_ge(w_mm, 2)
                for i in range(2):
                    dve.tensor_copy(wo_t2[:, :, i, :], fill[2][:, 0:256]).then_inc(w_dve, 1)
                dve.wait_ge(w_dve, 1)
                for i in range(2):
                    dve.tensor_scalar(qk_gamma[:, i::2, :], fill[i][:, :].rearrange("r (p c) -> r p c", p=HP),
                                      gamma_scaled[:, 0:1], None, ALU.mult).then_inc(w_dve, 1)
                dve.wait_ge(w_dve, 6)
                dve.tensor_copy(w_straight[:, :, :], qk_gamma[:, :, :]).then_inc(w_dve, 1)
                dve.tensor_copy(w_crossed[:, :, :], qk_gamma[:, :, :]).then_inc(w_dve, 1)
                dve.wait_ge(w_dve, 8)
                for w, r in ((w_straight, 64), (w_crossed, 0)):
                    dve.tensor_tensor(w[r:r + 64, :, :], qk_gamma[r:r + 64, :, :], w[r:r + 64, :, :].bitcast(F32),
                                      ALU.subtract).then_inc(w_dve, 1)
                dve.wait_ge(w_mm, 3)
                dve.tensor_scalar(d_part[:, :], misc[:, 0:H], SCALE, None, ALU.mult).then_inc(w_dve, 1)
                dve.wait_ge(w_dve, 11)
                dve.scalar_tensor_tensor(out=d_col[:, :], in0=misc[:, H:2 * H], scalar=SCALE, in1=d_part[:, :],
                                         op0=ALU.mult, op1=ALU.add).then_inc(w_dve, 1)
                dve.wait_ge(w_mm, 4)
                dve.tensor_copy(u_t[:, :, :], fill[3][:, 0:256]).then_inc(w_dve, 1)
                dve.wait_ge(w_mm, 5)
                dve.tensor_tensor(out_bias[:, :], z_bank[:, 0:1], bo2[:, :], ALU.add).then_inc(w_dve, 1)

            def copy_turned(pair, unit):
                wait(dve, probs_turned, pair.count(UNITS, unit + 1))
                hp = unit // (2 * PS)
                owner, older = of_step(pair, 2 * PS * hp - PROBS_T)
                if owner.exists():
                    wait(dve, z_summed, owner.count(HP, older // (2 * PS) + 1))
                dve.tensor_copy(probs_t[:, unit % PROBS_T, :, :], turned[unit % PT_BANKS][:, :]
                                ).then_inc(probs_t_dve, 1)

            def row_max(pair, unit):
                wait(dve, scored, pair.count(UNITS, unit + 1))
                dve.tensor_reduce(neg_max[:, unit, :],
                                  fill[bank_of("scores", unit)][:, :].rearrange("p (t k) -> p t k", t=QT),
                                  AX.X, ALU.max, negate=True).then_inc(max_ready, 1)

            def reciprocal(pair, unit):
                wait(dve, exp_ready, pair.count(UNITS, unit + 1))
                dve.reciprocal(recip[:, unit, :], denom[:, unit, :]).then_inc(recip_ready, 1)

            def t_lo(pair, h):
                wait(dve, t_hi_ready, pair.count(H, h + 1))
                half = t_stack[64:128, h, :, :]
                dve.scalar_tensor_tensor(out=half, in0=fill[bank_of("proj", h)][64:128, :], scalar=d_col[64:128, h:h + 1],
                                         in1=half.bitcast(F32), op0=ALU.add, op1=ALU.subtract
                                         ).then_inc(t_lo_ready, 1)

            def channel_moments(pair):
                p = pair.parity()
                wait(dve, x_loaded[p], pair.dma_count(1) * 2)
                for s in range(PS):
                    dve.bn_stats(moments[:, s, :], x2[p][:, s, :]).then_inc(moments_ready, 1)

            def channel_mean_var(pair):
                for s in range(PS):
                    dve.bn_aggr(mean_var[:, s, :], moments[:, s, :]).then_inc(mean_var_ready, 1)

            def channel_spread(pair):
                wait(dve, mean_summed, pair.count(1, 1))
                dve.tensor_copy(mean[:, :], misc[:, 0:PS]).then_inc(centred_ready, 1)
                dve.tensor_tensor(centred[:, :], mean_var[:, :, 0], misc[:, 0:PS], ALU.subtract
                                  ).then_inc(centred_ready, 1)
                wait(dve, centred_ready, pair.count(2, 2))
                dve.tensor_tensor(squared[:, :], centred[:, :], centred[:, :], ALU.mult).then_inc(squared_ready, 1)
                wait(dve, squared_ready, pair.count(1, 1))
                dve.tensor_tensor(spread[:, :], squared[:, :], mean_var[:, :, 1], ALU.add).then_inc(spread_ready, 1)

            def sample_variance(pair):
                wait(dve, var_summed, pair.count(1, 1))
                dve.tensor_scalar(variance[:, :], misc[:, PS:2 * PS], EPS, None, ALU.add).then_inc(variance_ready, 1)

            def normalise(pair):
                wait(dve, rstd_ready, pair.count(1, 1))
                if not isinstance(pair.j, int) or pair.c > 1:
                    wait(dve, projected, pair.count(H, -H))
                for s in range(PS):
                    dve.tensor_scalar(xhat[pair.parity()][:, s, :], x2[pair.parity()][:, s, :], mean[:, s:s + 1], rstd[:, s:s + 1],
                                      ALU.subtract, ALU.mult).then_inc(xhat_ready, 1)
                wait(dve, xhat_ready, pair.count(2, 2))
                dve.tensor_copy(x_stack[pair.parity()][:, :, :], xhat[pair.parity()][:, :, :]).then_inc(x_hi_ready, 1)

            def context_hi(pair):
                p = pair.parity()
                wait(dve, c_loaded[p], pair.dma_count(1) * 2)
                dve.tensor_copy(c_straight[p][0:64, :, :], c2[p][0:64, :, :]).then_inc(c_hi_ready, 1)
                dve.tensor_copy(c_crossed[p][64:128, :, :], c2[p][64:128, :, :]).then_inc(c_hi_ready, 1)

            def copy_ctx_t(pair):
                wait(dve, ctx_turned, pair.count(2, 2))
                wait(dve, z_summed, pair.count(HP, -HP))
                dve.tensor_copy(ctx_t[pair.parity()][:, :, :, :].rearrange("p s t c -> p (s t) c"),
                                misc[:, :].rearrange("p (n c) -> p n c", c=2 * CK)[:, :, 0:CK]
                                ).then_inc(ctx_t_ready, 1)

            def result(pair):
                p = pair.parity()
                wait(dve, out_summed, pair.count(1, 1))
                wait(dve, x_res_loaded[p], pair.dma_count(1))
                wait(dve, y_free[p], pair.dma_count(1))
                dve.scalar_tensor_tensor(out=y[p][:, :], in0=misc[:, 0:S], scalar=out_bias[:, 0:1], in1=x_res[p][:, :],
                                         op0=ALU.add, op1=ALU.add).then_inc(y_ready, 1)

            def steps(pair):
                for u in range(UNITS):
                    for h in range(H):
                        if owner := due(pair, u, T_LO_STEP[h]):
                            t_lo(owner, h)
                    owner, v = of_step(pair, u - 1)
                    if owner.exists() and v in DVE_EVACS:
                        copy_turned(owner, v)
                    if moments_owner := due(pair, u, MOMENTS_STEP):
                        channel_moments(moments_owner)
                        wait(dve, moments_ready, moments_owner.count(2, 2))
                    owner, v = of_step(pair, u + LEAD)
                    if owner.exists():
                        row_max(owner, v)
                    if moments_owner:
                        channel_mean_var(moments_owner)
                    owner, v = of_step(pair, u + LEAD - 2)
                    if owner.exists():
                        reciprocal(owner, v)
                    if owner := due(pair, u, SPREAD_STEP):
                        channel_spread(owner)
                    if owner := due(pair, u, RSTD_STEP):
                        sample_variance(owner)
                    if owner := due(pair, u, XHAT_STEP):
                        normalise(owner)
                    if owner := due(pair, u, C_HI_STEP):
                        context_hi(owner)
                    if owner := due(pair, u, CTX_COPY_STEP):
                        copy_ctx_t(owner)
                    if owner := due(pair, u, RESULT_STEP):
                        result(owner)

            weights()
            walk(dve, steps)

        @block.gpsimd
        def _(pool):
            pool.memset(bq_cols[:, :, :], 0.0).then_inc(consts_ready, 1)
            pool.memset(ident[:, :], 0.0).then_inc(consts_ready, 1)
            pool.memset(ones[:, :], 1.0 / 128).then_inc(consts_ready, 1)
            pool.memset(minus_half[:, :], -0.5).then_inc(consts_ready, 1)
            pool.wait_ge(consts_ready, 4)
            pool.affine_select(out=ident[:, :], in_=ident[:, :], compare_op=ALU.not_equal, fill=1.0, base=0,
                               pattern=[[-1, 128]], channel_multiplier=1).then_inc(consts_ready, 1)

            def divide(pair, unit):
                wait(pool, recip_ready, pair.count(UNITS, unit + 1))
                p = probs[:, unit % PROBS, :, :]
                pool.tensor_tensor(p, p, recip[:, unit, :].unsqueeze(2).broadcast_to([128, QT, K]), ALU.mult
                                   ).then_inc(probs_ready, 1)

            def inverse_root(pair):
                wait(pool, variance_ready, pair.count(1, 1))
                pool.tensor_tensor(rstd[:, :], variance[:, :], minus_half[:, :], ALU.pow).then_inc(rstd_ready, 1)

            def x_lo(pair):
                wait(pool, x_hi_ready, pair.count(1, 1))
                half = x_stack[pair.parity()][64:128, :, :]
                pool.tensor_tensor(half, xhat[pair.parity()][64:128, :, :], half.bitcast(F32), ALU.subtract).then_inc(x_stack_ready, 1)

            def context_lo(pair):
                p = pair.parity()
                wait(pool, c_hi_ready, pair.count(2, 2))
                pool.tensor_tensor(c_straight[p][64:128, :, :], c2[p][64:128, :, :],
                                   c_crossed[p][64:128, :, :].bitcast(F32), ALU.subtract).then_inc(c_lo_ready, 1)
                wait(pool, c_lo_ready, pair.count(2, 1))
                pool.tensor_tensor(c_crossed[p][0:64, :, :], c2[p][0:64, :, :],
                                   c_straight[p][0:64, :, :].bitcast(F32), ALU.subtract).then_inc(c_lo_ready, 1)

            def steps(pair):
                for u in range(UNITS):
                    divided, v = of_step(pair, u + LEAD - 2)
                    if divided.exists():
                        divide(divided, v)
                    if owner := due(pair, u, RSTD_STEP):
                        inverse_root(owner)
                    x_owner, c_owner = due(pair, u, X_LO_STEP), due(pair, u, C_LO_STEP)
                    if (x_owner or c_owner) and divided.exists():
                        wait(pool, probs_ready, divided.count(UNITS, v + 1))
                    if x_owner:
                        x_lo(x_owner)
                        wait(pool, x_stack_ready, x_owner.count(1, 1))
                    if c_owner:
                        context_lo(c_owner)
                        wait(pool, c_lo_ready, c_owner.count(2, 2))

            walk(pool, steps)


W_DVE = 14


_INS = ["x", "ctx_2048", "L0_xattn_gamma", "L0_xattn_beta", "L0_xattn_Wq", "L0_xattn_bq", "L0_xattn_Wkv",
        "L0_xattn_bkv", "L0_xattn_Wo", "L0_xattn_bo"]


def kernel(**inputs):
    import numpy as np
    import concourse.bacc as bacc
    from concourse.bass_utils import run_bass_kernel_spmd

    nc = bacc.Bacc("TRN2", target_bir_lowering=False, num_devices=1)
    arrays, args = {}, []
    for name in _INS:
        a = np.ascontiguousarray(inputs[name])
        arrays[f"in_{name}"] = a
        args.append(nc.dram_tensor(f"in_{name}", a.shape, mybir.dt.from_np(a.dtype), kind="ExternalInput").ap())
    args.append(nc.dram_tensor("out", (B, C, S), F32, kind="ExternalOutput").ap())
    build(nc, *args)
    r = run_bass_kernel_spmd(nc, [arrays], core_ids=[0])
    return r.results[0]["out"]
```

```python
from contextlib import ExitStack

import concourse.bass as bass
from concourse import mybir

F32 = mybir.dt.float32
F32R = mybir.dt.float32r
ALU = mybir.AluOpType
ACT = mybir.ActivationFunctionType
AX = mybir.AxisListType

B, C, S = 64, 64, 256
K, CK = 256, 64
H = 8
EPS = 1e-5
SCALE = float(C) ** -0.5

PS = 2
NPAIR = B // PS
UNITS = PS * H
QT = S // 128
KT = K // 128
HP = H // 2

FILL_BANKS = 4
PT_BANKS = 2
W_DVE = 11
PROBS = 8
PROBS_T = 8
DVE_EVACS = frozenset(range(0, UNITS, 2))



def every(kind, at, count, distance=1.0):
    return [(at + distance * i, kind, i) for i in range(count)]


PROJ, VALUES, DISTANCE = -8.57, -4.16, 1.87
PE_ORDER = (every("scores", -3.69, UNITS) + every("proj", PROJ, HP, 4) + every("turn", 1.26, UNITS)
            + every("attend", 4.1, H, PS) + every("values", VALUES, PS * KT, DISTANCE)
            + [(-13.42, "mean", 0), (-11.99, "var", 0)])
ACT_ORDER = (every("t_hi", PROJ + 0.21, HP, 4) + every("exp", -2.39, UNITS)
             + [work for work in every("copy", 1.27, UNITS) if work[2] not in DVE_EVACS]
             + every("values", VALUES + 0.38, PS * KT, DISTANCE))
DVE_ORDER = (every("t_lo", PROJ + 1.08, HP, 4) + every("max", -3.24, UNITS) + every("recip", -1.98, UNITS)
             + [work for work in every("copy", 0.93, UNITS) if work[2] in DVE_EVACS]
             + [(-15.75, "moments", 0), (-14.01, "mean_var", 0), (-13.2, "spread", 0),
                (-12.47, "sample_var", 0), (-11.46, "norm", 0), (-7.73, "c_hi", 0), (18.63, "result", 0)])
POOL_ORDER = every("divide", -1.67, UNITS) + [(-12.79, "root", 0), (-11.54, "x_lo", 0), (-7.21, "c_lo", 0)]
SYNC_ORDER = (every("t_hi", PROJ + 0.21 + 0.5, HP, 4) + every("t_lo", PROJ + 1.08 + 1.0, HP, 4)
              + [(-11.46 + 1.0, "load_x", 0), (-7.21 + 2.0, "load_c", 0), (8.5, "residual", 0),
                 (18.63 + 1.0, "store", 0)])


def in_order(order):
    return sorted(order, key=lambda work: work[0] % UNITS)


_kinds = [_kind for _, _kind, _ in in_order(DVE_ORDER)]
assert _kinds[(_kinds.index("moments") + 1) % len(_kinds)] != "mean_var"

FILLS = [(_kind, _item, _at) for _at, _kind, _item in in_order(PE_ORDER) if _kind in ("scores", "proj")]
NFILL = len(FILLS)
assert NFILL % FILL_BANKS == 0


def fill_of(kind, item):
    return [f[:2] for f in FILLS].index((kind, item))


def bank_of(kind, item):
    return fill_of(kind, item) % FILL_BANKS


class Pair:

    def __init__(self, j, c):
        self.j, self.c = j, c

    def shift(self, n):
        return Pair(self.j, self.c + n)

    def exists(self):
        return not isinstance(self.j, int) or 0 <= self.c < NPAIR

    def first(self):
        return isinstance(self.j, int) and self.c == 0

    def parity(self):
        return self.c % 2

    def count(self, per_pair, k):
        return self.j * (2 * per_pair) + (per_pair * self.c + k)

    def dma_count(self, k):
        return self.j * 16 + 16 * (self.c // 2 + k)

    def rows(self):
        return self.j * (2 * PS) + PS * self.c


def of_step(pair, item):
    return (pair.shift(item // UNITS), item % UNITS)


def work(pair, order):
    for at, kind, item in in_order(order):
        owner = pair.shift(-int(at // UNITS))
        if owner.exists():
            yield kind, item, owner


def wait(eng, sem, value):
    if not isinstance(value, int) or value > 0:
        eng.wait_ge(sem, value)


def on_both_halves(vector):
    return vector.unsqueeze(0).broadcast_to([2, C])


def walk(eng, steps):
    steps(Pair(0, -1))
    steps(Pair(0, 0))
    with eng.Fori(0, (NPAIR - 2) // 2) as j:
        steps(Pair(j, 1))
        steps(Pair(j, 2))
    steps(Pair(0, NPAIR - 1))
    steps(Pair(0, NPAIR))


def build(nc, x, ctx, gamma, beta, Wq, bq, Wkv, bkv, Wo, bo, out):
    stack = ExitStack()
    with stack:
        def sb(name, shape, dt=F32):
            return stack.enter_context(nc.sbuf_tensor(name, shape, dt))

        def pb(name, shape):
            return stack.enter_context(nc.psum_tensor(name, shape, F32))

        def sem(name):
            return stack.enter_context(nc.semaphore(name))

        wq2 = sb("wq2", [128, HP, 2, C])
        wk = sb("wk", [128, HP, CK])
        wv2 = sb("wv2", [128, HP, 2, CK])
        wo = sb("wo", [C, H * C])
        bq_col = sb("bq_col", [128, HP])
        bv_col = sb("bv_col", [128, HP])
        bo2 = sb("bo2", [128, 1])
        gamma2 = sb("gamma2", [128, 1])
        beta_col = sb("beta_col", [C, 1])
        gamma_scaled = sb("gamma_scaled", [128, 1])
        qk = sb("qk", [128, H, CK])
        qk_gamma = sb("qk_gamma", [128, H, CK])
        w_straight = sb("w_straight", [128, H, CK], F32R)
        w_crossed = sb("w_crossed", [128, H, CK], F32R)
        d_part = sb("d_part", [128, HP])
        d_col = sb("d_col", [128, HP])
        wo_t2 = sb("wo_t2", [128, HP, 2, C])
        u_t = sb("u_t", [128, H, C])
        u_straight = sb("u_straight", [128, H, C], F32R)
        u_crossed = sb("u_crossed", [128, H, C], F32R)
        out_bias = sb("out_bias", [128, 1])
        ident = sb("ident", [128, 128])
        ones = sb("ones", [128, 128])
        minus_half = sb("minus_half", [128, PS])
        x2 = [sb(f"x2_{i}", [128, PS, S]) for i in range(2)]
        c2 = [sb(f"c2_{i}", [128, PS, K]) for i in range(2)]
        x_res = [sb(f"x_res_{i}", [128, S]) for i in range(2)]
        moments = sb("moments", [128, PS, 6])
        mean_var = sb("mean_var", [128, PS, 2])
        mean = sb("mean", [128, PS])
        centred = sb("centred", [128, PS])
        squared = sb("squared", [128, PS])
        spread = sb("spread", [128, PS])
        variance = sb("variance", [128, PS])
        rstd = sb("rstd", [128, PS])
        xhat = [sb(f"xhat_{i}", [128, PS, S]) for i in range(2)]
        x_stack = [sb(f"x_stack_{i}", [128, PS, S], F32R) for i in range(2)]
        c_straight = [sb(f"c_straight_{i}", [128, PS, K], F32R) for i in range(2)]
        c_crossed = [sb(f"c_crossed_{i}", [128, PS, K], F32R) for i in range(2)]
        values = [sb(f"values_{i}", [128, PS, KT, H, C]) for i in range(2)]
        t_up = sb("t_up", [128, HP, PS, S], F32R)
        t_low = sb("t_low", [128, HP, PS, S], F32R)
        t_stack = sb("t_stack", [128, H, PS, S], F32R)
        neg_max = sb("neg_max", [128, UNITS, QT])
        denom = sb("denom", [128, UNITS, QT])
        recip = sb("recip", [128, UNITS, QT])
        probs = sb("probs", [128, PROBS, QT, K])
        probs_t = sb("probs_t", [128, PROBS_T, KT, S])
        y = [sb(f"y_{i}", [128, S]) for i in range(2)]

        fill = [pb(f"fill_{i}", [128, 512]) for i in range(FILL_BANKS)]
        turned = [pb(f"turned_{i}", [128, 512]) for i in range(PT_BANKS)]
        out_bank = pb("out_bank", [128, 512])
        misc = pb("misc", [128, 512])

        qk_loaded = sem("qk_loaded")
        weights_loaded = sem("weights_loaded")
        x_loaded = [sem(f"x_loaded_{i}") for i in range(2)]
        c_loaded = [sem(f"c_loaded_{i}") for i in range(2)]
        x_res_loaded = [sem(f"x_res_loaded_{i}") for i in range(2)]
        y_free = [sem(f"y_free_{i}") for i in range(2)]
        consts_ready = sem("consts_ready")
        w_mm = sem("w_mm")
        w_act = sem("w_act")
        w_dve = sem("w_dve")
        moments_ready = sem("moments_ready")
        mean_var_ready = sem("mean_var_ready")
        mean_summed = sem("mean_summed")
        centred_ready = sem("centred_ready")
        squared_ready = sem("squared_ready")
        spread_ready = sem("spread_ready")
        var_summed = sem("var_summed")
        variance_ready = sem("variance_ready")
        rstd_ready = sem("rstd_ready")
        xhat_ready = sem("xhat_ready")
        x_hi_ready = sem("x_hi_ready")
        x_stack_ready = sem("x_stack_ready")
        c_hi_ready = sem("c_hi_ready")
        c_lo_ready = sem("c_lo_ready")
        projected = sem("projected")
        t_hi_ready = sem("t_hi_ready")
        t_lo_ready = sem("t_lo_ready")
        t_stacked = [sem(f"t_stacked_{i}") for i in range(HP)]
        scored = sem("scored")
        max_ready = sem("max_ready")
        exp_ready = sem("exp_ready")
        recip_ready = sem("recip_ready")
        probs_ready = sem("probs_ready")
        probs_turned = sem("probs_turned")
        probs_t_act = sem("probs_t_act")
        probs_t_dve = sem("probs_t_dve")
        values_summed = sem("values_summed")
        values_ready = sem("values_ready")
        attended = sem("attended")
        y_ready = sem("y_ready")

        ACT_EVACS = [u for u in range(UNITS) if u not in DVE_EVACS]

        def probs_t_wait(eng, pair, unit):
            if unit in DVE_EVACS:
                order = sorted(DVE_EVACS)
                wait(eng, probs_t_dve, pair.count(len(order), order.index(unit) + 1))
            else:
                wait(eng, probs_t_act, pair.count(len(ACT_EVACS), ACT_EVACS.index(unit) + 1))

        qk_weights = [(gamma2[:, :], on_both_halves(gamma))] + [
            (wq2[:, :, i, :], Wq.rearrange("(p r) c -> r p c", r=128)) for i in range(2)]
        out_weights = [(wo[:, :], Wo), (bv_col[:, :], bkv[H * C:2 * H * C].rearrange("(p r) -> r p", r=128)),
                       (bo2[:, :], on_both_halves(bo))]
        k_weights = [(wk[:, :, :], Wkv[0:H * C, :].rearrange("(p r) c -> r p c", r=128))]
        v_weights = [(beta_col[:, :], beta.unsqueeze(1)), (bq_col[:, :], bq.rearrange("(p r) -> r p", r=128))] + [
            (wv2[:, :, i, :], Wkv[H * C:2 * H * C, :].rearrange("(p r) c -> r p c", r=128)) for i in range(2)]
        QK_DMAS = len(qk_weights) + len(k_weights)
        OTHER_DMAS = len(out_weights) + len(v_weights)

        def load_weights(eng, weights, loaded):
            for dst, src in weights:
                eng.dma_start(dst, src, allow_slow_non_contiguous=True).then_inc(loaded, 16)

        block = stack.enter_context(nc.Block())

        @block.sync
        def _(sync):
            def load_x(pair, row):
                p = pair.parity()
                src = x[bass.ds(row, PS), :, :].rearrange("s c q -> c s q")
                for half in range(2):
                    sync.dma_start(x2[p][64 * half:64 * half + 64, :, :], src).then_inc(x_loaded[p], 16)

            def load_c(pair, row):
                p = pair.parity()
                src = ctx[bass.ds(row, PS), :, :].rearrange("s c q -> c s q")
                for half in range(2):
                    sync.dma_start(c2[p][64 * half:64 * half + 64, :, :], src).then_inc(c_loaded[p], 16)

            load_x(Pair(0, 0), 0)
            for p in range(2):
                sync.sem_inc(y_free[p], 16)
            load_weights(sync, k_weights, qk_loaded)
            load_c(Pair(0, 0), 0)
            load_weights(sync, v_weights, weights_loaded)
            load_x(Pair(0, 1), 2)
            load_c(Pair(0, 1), 2)

            def steps(pair):
                rows = {}
                for kind, item, owner in work(pair, SYNC_ORDER):
                    if kind not in ("t_hi", "t_lo"):
                        row = (owner.shift(2) if kind.startswith("load") else owner).rows()
                        rows[kind] = row if isinstance(row, int) else sync.snap(row)
                for kind, item, owner in work(pair, SYNC_ORDER):
                    p = owner.parity()
                    if kind == "load_x" and owner.shift(2).exists():
                        wait(sync, xhat_ready, owner.count(2, 2))
                        load_x(owner.shift(2), rows[kind])
                    elif kind == "load_c" and owner.shift(2).exists():
                        wait(sync, c_lo_ready, owner.count(2, 2))
                        load_c(owner.shift(2), rows[kind])
                    elif kind == "residual":
                        wait(sync, attended, owner.count(H, 1 - H))
                        sync.dma_start(x_res[p][:, :], x[bass.ds(rows[kind], PS), :, :].rearrange("s c q -> (s c) q")
                                       ).then_inc(x_res_loaded[p], 16)
                    elif kind == "store":
                        wait(sync, y_ready, owner.count(1, 1))
                        sync.dma_start(out[bass.ds(rows[kind], PS), :, :].rearrange("s c q -> (s c) q"),
                                       y[p][:, :]).then_inc(y_free[p], 16)
                    elif kind == "t_hi":
                        wait(sync, t_hi_ready, owner.count(HP, item + 1))
                        for o in range(2):
                            sync.dma_start(t_stack[0:64, 2 * item + o, :, :].bitcast(F32),
                                           t_up[64 * o:64 * o + 64, item, :, :].bitcast(F32)).then_inc(t_stacked[item], 16)
                    elif kind == "t_lo":
                        wait(sync, t_lo_ready, owner.count(HP, item + 1))
                        for o in range(2):
                            sync.dma_start(t_stack[64:128, 2 * item + o, :, :].bitcast(F32),
                                           t_low[64 * o:64 * o + 64, item, :, :].bitcast(F32)).then_inc(t_stacked[item], 16)

            for c in (-1, 0):
                steps(Pair(0, c))
            with sync.Fori(0, (NPAIR - 4) // 2) as j:
                steps(Pair(j, 1))
                steps(Pair(j, 2))
            for c in range(NPAIR - 3, NPAIR + 1):
                steps(Pair(0, c))
            for p in range(2):
                sync.wait_ge(y_free[p], 16 * (NPAIR // 2 + 1))

        @block.tensor
        def _(pe):
            def query_key_products():
                pe.wait_ge(qk_loaded, 16 * QK_DMAS)
                for h in range(H):
                    r = 64 * (h % 2)
                    mm = pe.matmul(fill[h % 2][:, CK * (h // 2):CK * (h // 2) + CK],
                                   wq2[r:r + 64, h // 2, :, :], wk[r:r + 64, h // 2, :], start=True, stop=True)
                mm.then_inc(w_mm, 1)
                pe.wait_ge(weights_loaded, 16 * OTHER_DMAS)
                for p in range(HP):
                    mm = pe.transpose(turned[0][:, C * p:C * p + C], wo[:, 128 * p:128 * p + 128], ident[0:64, 0:64])
                mm.then_inc(w_mm, 1)
                pe.wait_ge(w_act, 3)
                for p in range(HP):
                    pe.matmul(turned[1][:, p:p + 1], qk[0:64, 2 * p:2 * p + 2, :], beta_col[:, :], start=True, stop=True)
                for p in range(HP):
                    for r in (0, 64):
                        mm = pe.matmul(turned[1][r:r + 64, HP + p:HP + p + 1], wk[r:r + 64, p, :],
                                       bq_col[r:r + 64, p:p + 1], start=True, stop=True)
                mm.then_inc(w_mm, 1)
                pe.wait_ge(w_dve, 4)

            def output_value_products():
                pe.wait_ge(w_act, 6)
                pe.wait_ge(w_dve, 6)
                for h in range(H):
                    r = 64 * (h % 2)
                    mm = pe.matmul(turned[h % 2][:, C * (h // 2):C * (h // 2) + C],
                                   wv2[r:r + 64, h // 2, :, :], wo_t2[r:r + 64, h // 2, 0, :], start=True, stop=True)
                mm.then_inc(w_mm, 1)
                for p in range(HP):
                    mm = pe.matmul(out_bank[:, 0:1], wo_t2[:, p, :, :], bv_col[:, p:p + 1],
                                   start=(p == 0), stop=(p == HP - 1))
                mm.then_inc(w_mm, 1)

            def free_bank(pair, k):
                k -= FILL_BANKS
                if k < 0:
                    pair, k = pair.shift(-1), k + NFILL
                kind, item, step = FILLS[k]
                owner = pair.shift(-int(step // UNITS))
                if owner.exists():
                    if kind == "scores":
                        wait(pe, exp_ready, owner.count(UNITS, item + 1))
                    else:
                        wait(pe, t_lo_ready, owner.count(HP, item + 1))

            def scores(pair, v, bank):
                h, s, p = v // PS, v % PS, pair.parity()
                for qt in range(QT):
                    lhs = t_stack[:, h, s, 128 * qt:128 * qt + 128]
                    dst = bank[:, K * qt:K * qt + K]
                    pe.matmul(dst, lhs, c_straight[p][:, s, :], start=True, stop=False)
                    mm = pe.matmul(dst, lhs, c_crossed[p][:, s, :], start=False, stop=True)
                mm.then_inc(scored, 1)

            def project(pair, hp, bank):
                xs = x_stack[pair.parity()][:, :, :]
                pe.matmul(bank[:, :], w_straight[:, 2 * hp:2 * hp + 2, :], xs, start=True, stop=False)
                pe.matmul(bank[:, :], w_crossed[:, 2 * hp:2 * hp + 2, :], xs, start=False, stop=True).then_inc(projected, 1)

            def fill_bank(pair, kind, item, owner):
                k = fill_of(kind, item)
                free_bank(pair, k)
                if kind == "scores":
                    if item == 0:
                        wait(pe, c_lo_ready, owner.count(2, 2))
                    if item % (2 * PS) == 0:
                        wait(pe, t_stacked[item // (2 * PS)], owner.count(64, 64))
                    scores(owner, item, fill[k % FILL_BANKS])
                else:
                    if item == 0:
                        wait(pe, x_stack_ready, owner.count(1, 1))
                    project(owner, item, fill[k % FILL_BANKS])

            def turn_probs(pair, unit):
                wait(pe, probs_ready, pair.count(UNITS, unit + 1))
                owner, v = of_step(pair, unit - PT_BANKS)
                if owner.exists():
                    probs_t_wait(pe, owner, v)
                for kt in range(KT):
                    for qt in range(QT):
                        mm = pe.transpose(turned[unit % PT_BANKS][:, S * kt + 128 * qt:S * kt + 128 * qt + 128],
                                          probs[:, unit % PROBS, qt, 128 * kt:128 * kt + 128], ident[:, :])
                mm.then_inc(probs_turned, 1)

            def attend(pair, h):
                units = [PS * h + s for s in range(PS)]
                for unit in units:
                    probs_t_wait(pe, pair, unit)
                if h == 0:
                    wait(pe, values_ready, pair.count(PS * KT, PS * KT))
                    wait(pe, y_ready, pair.count(1, 0))
                for kt in range(KT):
                    for s in range(PS):
                        mm = pe.matmul(out_bank[64 * s:64 * s + 64, 0:S], values[pair.parity()][:, s, kt, h, :],
                                       probs_t[:, units[s] % PROBS_T, kt, :],
                                       start=(h == 0 and kt == 0), stop=(h == H - 1 and kt == KT - 1))
                mm.then_inc(attended, 1)

            def make_values(pair, i):
                s, kt = i // KT, i % KT
                if i == 0:
                    wait(pe, c_lo_ready, pair.count(2, 2))
                    wait(pe, variance_ready, pair.count(1, 1))
                    if pair.first():
                        pe.wait_ge(w_dve, W_DVE)
                else:
                    wait(pe, values_ready, pair.count(PS * KT, i))
                lhs = c_straight[pair.parity()][:, s, 128 * kt:128 * kt + 128]
                pe.matmul(misc[:, :], lhs, u_straight[:, :, :], start=True, stop=False)
                pe.matmul(misc[:, :], lhs, u_crossed[:, :, :], start=False, stop=True).then_inc(values_summed, 1)

            def sum_means(pair):
                wait(pe, mean_var_ready, pair.count(2, 2))
                wait(pe, values_ready, pair.count(PS * KT, 0))
                pe.matmul(misc[:, 0:PS], ones[:, :], mean_var[:, :, 0], start=True, stop=True
                          ).then_inc(mean_summed, 1)

            def sum_spreads(pair):
                wait(pe, spread_ready, pair.count(1, 1))
                pe.matmul(misc[:, PS:2 * PS], ones[:, :], spread[:, :], start=True, stop=True
                          ).then_inc(var_summed, 1)

            def steps(pair):
                for kind, item, owner in work(pair, PE_ORDER):
                    if kind == "proj" and owner.first():
                        if item == 0:
                            query_key_products()
                        elif item == 1:
                            output_value_products()
                    if kind in ("scores", "proj"):
                        fill_bank(pair, kind, item, owner)
                    elif kind == "turn":
                        turn_probs(owner, item)
                    elif kind == "attend":
                        attend(owner, item)
                    elif kind == "values":
                        make_values(owner, item)
                    elif kind == "mean":
                        sum_means(owner)
                    else:
                        sum_spreads(owner)

            pe.wait_ge(consts_ready, 4)
            walk(pe, steps)

        @block.scalar
        def _(act):
            def query_key_steps():
                act.wait_ge(qk_loaded, 16 * QK_DMAS)
                act.mul(gamma_scaled[:, :], gamma2[:, :], SCALE).then_inc(w_act, 1)
                act.wait_ge(w_mm, 1)
                for i in range(2):
                    act.copy(qk[:, i::2, :], fill[i][:, 0:HP * CK].rearrange("r (p c) -> r p c", p=HP)
                             ).then_inc(w_act, 1)
                act.wait_ge(w_dve, 1)
                act.copy(w_crossed[:, :, :], qk_gamma[:, :, :]).then_inc(w_act, 1)
                act.wait_ge(w_mm, 2)
                for i in range(2):
                    act.copy(wo_t2[:, :, i, :], turned[0][:, 0:HP * C].rearrange("r (p c) -> r p c", p=HP)
                             ).then_inc(w_act, 1)
                act.wait_ge(w_dve, 6)

            def output_value_steps():
                act.wait_ge(w_mm, 4)
                for i in range(2):
                    act.copy(u_t[:, i::2, :], turned[i][:, 0:HP * C].rearrange("r (p c) -> r p c", p=HP)
                             ).then_inc(w_act, 1)

            def copy_turned(pair, unit):
                wait(act, probs_turned, pair.count(UNITS, unit + 1))
                owner, older = of_step(pair, unit - PROBS_T)
                if owner.exists():
                    wait(act, attended, owner.count(H, older // PS + 1))
                act.copy(probs_t[:, unit % PROBS_T, :, :], turned[unit % PT_BANKS][:, :]
                         ).then_inc(probs_t_act, 1)

            def exponentials(pair, unit):
                bank = fill[bank_of("scores", unit)]
                wait(act, max_ready, pair.count(UNITS, unit + 1))
                wait(act, probs_turned, pair.count(UNITS, unit + 1 - PROBS))
                for qt in range(QT):
                    ins = act.activation(probs[:, unit % PROBS, qt, :], bank[:, K * qt:K * qt + K], ACT.Exp,
                                         bias=neg_max[:, unit, qt:qt + 1], accum_out=denom[:, unit, qt:qt + 1])
                ins.then_inc(exp_ready, 1)

            def t_hi(pair, hp):
                wait(act, projected, pair.count(HP, hp + 1))
                if pair.shift(-1).exists():
                    wait(act, scored, pair.shift(-1).count(UNITS, 2 * PS * (hp + 1)))
                act.activation(t_up[:, hp, :, :], fill[bank_of("proj", hp)][:, :], ACT.Identity,
                               bias=d_col[:, hp:hp + 1]).then_inc(t_hi_ready, 1)

            def copy_values(pair, i):
                wait(act, values_summed, pair.count(PS * KT, i + 1))
                if i == 0:
                    wait(act, attended, pair.count(H, -H))
                act.copy(values[pair.parity()][:, i // KT, i % KT, :, :], misc[:, :]).then_inc(values_ready, 1)

            def steps(pair):
                for kind, item, owner in work(pair, ACT_ORDER):
                    if kind == "t_hi" and owner.first():
                        if item == 0:
                            query_key_steps()
                        elif item == 1:
                            output_value_steps()
                    if kind == "t_hi":
                        t_hi(owner, item)
                    elif kind == "exp":
                        exponentials(owner, item)
                    elif kind == "copy":
                        copy_turned(owner, item)
                    else:
                        copy_values(owner, item)

            load_weights(act, qk_weights, qk_loaded)
            load_weights(act, out_weights, weights_loaded)
            walk(act, steps)

        @block.vector
        def _(dve):
            def query_key_steps():
                dve.wait_ge(w_act, 3)
                dve.tensor_scalar(qk_gamma[:, :, :], qk[:, :, :], gamma_scaled[:, 0:1], None, ALU.mult
                                  ).then_inc(w_dve, 1)
                dve.wait_ge(w_dve, 1)
                dve.tensor_copy(w_straight[:, :, :], qk_gamma[:, :, :]).then_inc(w_dve, 1)
                dve.wait_ge(w_dve, 2)
                dve.wait_ge(w_act, 4)
                for w, r in ((w_straight, 64), (w_crossed, 0)):
                    dve.tensor_tensor(w[r:r + 64, :, :], qk_gamma[r:r + 64, :, :], w[r:r + 64, :, :].bitcast(F32),
                                      ALU.subtract).then_inc(w_dve, 1)
                dve.wait_ge(w_mm, 3)
                dve.tensor_scalar(d_part[:, :], turned[1][:, 0:HP], SCALE, None, ALU.mult).then_inc(w_dve, 1)
                dve.wait_ge(w_dve, 5)
                dve.scalar_tensor_tensor(out=d_col[:, :], in0=turned[1][:, HP:2 * HP], scalar=SCALE, in1=d_part[:, :],
                                         op0=ALU.mult, op1=ALU.add).then_inc(w_dve, 1)

            def output_value_steps():
                dve.wait_ge(w_act, 8)
                dve.tensor_copy(u_straight[:, :, :], u_t[:, :, :]).then_inc(w_dve, 1)
                dve.tensor_copy(u_crossed[:, :, :], u_t[:, :, :]).then_inc(w_dve, 1)
                dve.wait_ge(w_dve, 8)
                for u, r in ((u_straight, 64), (u_crossed, 0)):
                    dve.tensor_tensor(u[r:r + 64, :, :], u_t[r:r + 64, :, :], u[r:r + 64, :, :].bitcast(F32),
                                      ALU.subtract).then_inc(w_dve, 1)
                dve.wait_ge(w_mm, 5)
                dve.tensor_tensor(out_bias[:, :], out_bank[:, 0:1], bo2[:, :], ALU.add).then_inc(w_dve, 1)

            def copy_turned(pair, unit):
                wait(dve, probs_turned, pair.count(UNITS, unit + 1))
                owner, older = of_step(pair, unit - PROBS_T)
                if owner.exists():
                    wait(dve, attended, owner.count(H, older // PS + 1))
                dve.tensor_copy(probs_t[:, unit % PROBS_T, :, :], turned[unit % PT_BANKS][:, :]
                                ).then_inc(probs_t_dve, 1)

            def row_max(pair, unit):
                wait(dve, scored, pair.count(UNITS, unit + 1))
                dve.tensor_reduce(neg_max[:, unit, :],
                                  fill[bank_of("scores", unit)][:, :].rearrange("p (t k) -> p t k", t=QT),
                                  AX.X, ALU.max, negate=True).then_inc(max_ready, 1)

            def reciprocal(pair, unit):
                wait(dve, exp_ready, pair.count(UNITS, unit + 1))
                dve.reciprocal(recip[:, unit, :], denom[:, unit, :]).then_inc(recip_ready, 1)

            def t_lo(pair, hp):
                wait(dve, t_hi_ready, pair.count(HP, hp + 1))
                dve.scalar_tensor_tensor(out=t_low[:, hp, :, :], in0=fill[bank_of("proj", hp)][:, :],
                                         scalar=d_col[:, hp:hp + 1], in1=t_up[:, hp, :, :].bitcast(F32), op0=ALU.add, op1=ALU.subtract
                                         ).then_inc(t_lo_ready, 1)

            def channel_moments(pair):
                p = pair.parity()
                wait(dve, x_loaded[p], pair.dma_count(1) * 2)
                for s in range(PS):
                    dve.bn_stats(moments[:, s, :], x2[p][:, s, :]).then_inc(moments_ready, 1)

            def channel_mean_var(pair):
                for s in range(PS):
                    dve.bn_aggr(mean_var[:, s, :], moments[:, s, :]).then_inc(mean_var_ready, 1)

            def channel_spread(pair):
                wait(dve, mean_summed, pair.count(1, 1))
                dve.tensor_copy(mean[:, :], misc[:, 0:PS]).then_inc(centred_ready, 1)
                dve.tensor_tensor(centred[:, :], mean_var[:, :, 0], misc[:, 0:PS], ALU.subtract
                                  ).then_inc(centred_ready, 1)
                wait(dve, centred_ready, pair.count(2, 2))
                dve.tensor_tensor(squared[:, :], centred[:, :], centred[:, :], ALU.mult).then_inc(squared_ready, 1)
                wait(dve, squared_ready, pair.count(1, 1))
                dve.tensor_tensor(spread[:, :], squared[:, :], mean_var[:, :, 1], ALU.add).then_inc(spread_ready, 1)

            def sample_variance(pair):
                wait(dve, var_summed, pair.count(1, 1))
                dve.tensor_scalar(variance[:, :], misc[:, PS:2 * PS], EPS, None, ALU.add).then_inc(variance_ready, 1)

            def normalise(pair):
                wait(dve, rstd_ready, pair.count(1, 1))
                if not isinstance(pair.j, int) or pair.c > 1:
                    wait(dve, projected, pair.count(HP, -HP))
                for s in range(PS):
                    dve.tensor_scalar(xhat[pair.parity()][:, s, :], x2[pair.parity()][:, s, :],
                                      mean[:, s:s + 1], rstd[:, s:s + 1], ALU.subtract, ALU.mult).then_inc(xhat_ready, 1)
                wait(dve, xhat_ready, pair.count(2, 2))
                dve.tensor_copy(x_stack[pair.parity()][:, :, :], xhat[pair.parity()][:, :, :]).then_inc(x_hi_ready, 1)

            def context_hi(pair):
                p = pair.parity()
                wait(dve, c_loaded[p], pair.dma_count(1) * 2)
                dve.tensor_copy(c_straight[p][0:64, :, :], c2[p][0:64, :, :]).then_inc(c_hi_ready, 1)
                dve.tensor_copy(c_crossed[p][64:128, :, :], c2[p][64:128, :, :]).then_inc(c_hi_ready, 1)

            def result(pair):
                p = pair.parity()
                wait(dve, attended, pair.count(H, H))
                wait(dve, x_res_loaded[p], pair.dma_count(1))
                wait(dve, y_free[p], pair.dma_count(1))
                dve.scalar_tensor_tensor(out=y[p][:, :], in0=out_bank[:, 0:S], scalar=out_bias[:, 0:1], in1=x_res[p][:, :],
                                         op0=ALU.add, op1=ALU.add).then_inc(y_ready, 1)

            def steps(pair):
                for kind, item, owner in work(pair, DVE_ORDER):
                    if kind == "t_lo" and owner.first():
                        if item == 0:
                            query_key_steps()
                        elif item == 1:
                            output_value_steps()
                    if kind == "t_lo":
                        t_lo(owner, item)
                    elif kind == "copy":
                        copy_turned(owner, item)
                    elif kind == "max":
                        row_max(owner, item)
                    elif kind == "recip":
                        reciprocal(owner, item)
                    elif kind == "moments":
                        channel_moments(owner)
                        wait(dve, moments_ready, owner.count(2, 2))
                    elif kind == "mean_var":
                        channel_mean_var(owner)
                    elif kind == "spread":
                        channel_spread(owner)
                    elif kind == "sample_var":
                        sample_variance(owner)
                    elif kind == "norm":
                        normalise(owner)
                    elif kind == "c_hi":
                        context_hi(owner)
                    else:
                        result(owner)

            walk(dve, steps)

        @block.gpsimd
        def _(pool):
            pool.memset(ident[:, :], 0.0).then_inc(consts_ready, 1)
            pool.memset(ones[:, :], 1.0 / 128).then_inc(consts_ready, 1)
            pool.memset(minus_half[:, :], -0.5).then_inc(consts_ready, 1)
            pool.wait_ge(consts_ready, 3)
            pool.affine_select(out=ident[:, :], in_=ident[:, :], compare_op=ALU.not_equal, fill=1.0, base=0,
                               pattern=[[-1, 128]], channel_multiplier=1).then_inc(consts_ready, 1)

            def divide(pair, unit):
                wait(pool, recip_ready, pair.count(UNITS, unit + 1))
                p = probs[:, unit % PROBS, :, :]
                pool.tensor_tensor(p, p, recip[:, unit, :].unsqueeze(2).broadcast_to([128, QT, K]), ALU.mult
                                   ).then_inc(probs_ready, 1)

            def inverse_root(pair):
                wait(pool, variance_ready, pair.count(1, 1))
                pool.tensor_tensor(rstd[:, :], variance[:, :], minus_half[:, :], ALU.pow).then_inc(rstd_ready, 1)

            def x_lo(pair):
                wait(pool, x_hi_ready, pair.count(1, 1))
                half = x_stack[pair.parity()][64:128, :, :]
                pool.tensor_tensor(half, xhat[pair.parity()][64:128, :, :], half.bitcast(F32), ALU.subtract
                                   ).then_inc(x_stack_ready, 1)

            def context_lo(pair):
                p = pair.parity()
                wait(pool, c_hi_ready, pair.count(2, 2))
                pool.tensor_tensor(c_straight[p][64:128, :, :], c2[p][64:128, :, :],
                                   c_crossed[p][64:128, :, :].bitcast(F32), ALU.subtract).then_inc(c_lo_ready, 1)
                wait(pool, c_lo_ready, pair.count(2, 1))
                pool.tensor_tensor(c_crossed[p][0:64, :, :], c2[p][0:64, :, :],
                                   c_straight[p][0:64, :, :].bitcast(F32), ALU.subtract).then_inc(c_lo_ready, 1)

            def steps(pair):
                done = None
                for kind, item, owner in work(pair, POOL_ORDER):
                    if kind in ("x_lo", "c_lo") and done:
                        wait(pool, probs_ready, done[0].count(UNITS, done[1] + 1))
                    if kind == "divide":
                        divide(owner, item)
                        done = owner, item
                    elif kind == "root":
                        inverse_root(owner)
                    elif kind == "x_lo":
                        x_lo(owner)
                        wait(pool, x_stack_ready, owner.count(1, 1))
                    else:
                        context_lo(owner)
                        wait(pool, c_lo_ready, owner.count(2, 2))

            walk(pool, steps)


_INS = ["x", "ctx_2048", "L0_xattn_gamma", "L0_xattn_beta", "L0_xattn_Wq", "L0_xattn_bq", "L0_xattn_Wkv",
        "L0_xattn_bkv", "L0_xattn_Wo", "L0_xattn_bo"]


def kernel(**inputs):
    import numpy as np
    import concourse.bacc as bacc
    from concourse.bass_utils import run_bass_kernel_spmd

    nc = bacc.Bacc("TRN2", target_bir_lowering=False, num_devices=1)
    arrays, args = {}, []
    for name in _INS:
        a = np.ascontiguousarray(inputs[name])
        arrays[f"in_{name}"] = a
        args.append(nc.dram_tensor(f"in_{name}", a.shape, mybir.dt.from_np(a.dtype), kind="ExternalInput").ap())
    args.append(nc.dram_tensor("out", (B, C, S), F32, kind="ExternalOutput").ap())
    build(nc, *args)
    r = run_bass_kernel_spmd(nc, [arrays], core_ids=[0])
    return r.results[0]["out"]
```
